# Optimizing a Trainium2 kernel written in Bass

```python
import numpy as np
import jax
import jax.numpy as jnp

def _softmax(x, axis=-1):
    return jax.nn.softmax(x, axis=axis)

def _gelu(x):
    return jax.nn.gelu(x, approximate=True)

def _silu(x):
    return jax.nn.silu(x)

def _sigmoid(x):
    return jax.nn.sigmoid(x)

def _layernorm(x, axis=-1, eps=1e-05):
    m = jnp.mean(x, axis=axis, keepdims=True)
    v = jnp.var(x, axis=axis, keepdims=True)
    return (x - m) / jnp.sqrt(v + eps)

def _scatter_add(tgt, idx, src, axis=0):
    return tgt.at[idx].add(src)

def _segment_sum(src, seg, n):
    return jax.ops.segment_sum(src, seg, n)
kernel_name = 'mk_adaln_ffn_d2_seqx_r4_a1afc7'

def setup_inputs(seed: int=0):
    np.random.seed(seed)
    _w = jnp.asarray

    def _rec_inputs():
        import jax
        import jax.numpy as jnp
        _rk = jax.random.key(seed)
        x = -0.000125 + 0.9999 * jax.random.normal(jax.random.fold_in(_rk, 1), (32, 64, 1024), jnp.float32)
        _lenS = 64 - jax.random.randint(jax.random.fold_in(_rk, 7), (32,), 0, max(1, 64 // 4) + 1, jnp.int32)
        _lenS2 = 64 - jax.random.randint(jax.random.fold_in(_rk, 8), (32,), 0, max(1, 64 // 4) + 1, jnp.int32)
        cond_128 = 0.0061147 + 1.02565 * jax.random.normal(jax.random.fold_in(_rk, 11), (32, 128), jnp.float32)
        fside_S_0 = -0.022604 + 0.987366 * jax.random.normal(jax.random.fold_in(_rk, 12), (64,), jnp.float32)
        return (x, cond_128, fside_S_0)
    x, cond_128, fside_S_0 = _rec_inputs()

    def _L0_cond_setup():
        import jax, jax.numpy as jnp
        import numpy as np
        from jax import lax
        N, C_IN, L = (32, 64, 1024)
        C_OUT, K, GROUPS = (64, 9, 4)
        C_DIM, PAD, STRIDE = (128, 4, 1)
        key = jax.random.key(seed)
        k1, k2, k3, k4, k5 = jax.random.split(key, 5)
        x = jax.random.normal(k1, (N, C_IN, L), dtype=jnp.float32)
        c = jax.random.normal(k2, (N, C_DIM), dtype=jnp.float32)
        weight = jax.random.normal(k3, (C_OUT, C_IN // GROUPS, K), dtype=jnp.float32)
        c_weight = jax.random.normal(k4, (C_OUT, C_DIM), dtype=jnp.float32)
        bias = jax.random.normal(k5, (C_OUT,), dtype=jnp.float32)
        return {'x': x, 'c': c, 'weight': weight, 'c_weight': c_weight, 'bias': bias}
    _L0_cond_all = _L0_cond_setup()
    _L0_cond_in = {k: v for k, v in _L0_cond_all.items() if k in ('weight', 'c_weight')}
    del _L0_cond_all

    def _L0_ffn_setup():
        import jax, jax.numpy as jnp
        import numpy as np
        LORA_RANK = 16
        LORA_ALPHA = 16
        LORA_SCALE = LORA_ALPHA / LORA_RANK
        key = jax.random.key(seed)
        k1, k2, k3, k4, k5 = jax.random.split(key, 5)
        B, S, D_IN, D_OUT, N_LORA, R = (8, 512, 1024, 1024, 3, LORA_RANK)
        std = 1.0 / np.sqrt(D_IN)
        x = jax.random.normal(k1, (B, S, D_IN), dtype=jnp.float32)
        weight = jax.random.truncated_normal(k2, -3.0, 3.0, (D_OUT, D_IN), dtype=jnp.float32) * std
        bias = jax.random.normal(k3, (D_OUT,), dtype=jnp.float32) * 0.01
        lora_A = jax.random.normal(k4, (N_LORA, R, D_IN), dtype=jnp.float32) * std
        lora_B = jax.random.normal(k5, (N_LORA, D_OUT, R), dtype=jnp.float32) * 0.02
        lora_start_indices = jnp.arange(4, dtype=jnp.int64) * 2
        return {'x': x, 'weight': weight, 'bias': bias, 'lora_A': lora_A, 'lora_B': lora_B, 'lora_start_indices': lora_start_indices}
    _L0_ffn_all = _L0_ffn_setup()
    _L0_ffn_in = {k: v for k, v in _L0_ffn_all.items() if k in ('weight', 'bias', 'lora_A', 'lora_B', 'lora_start_indices')}
    del _L0_ffn_all

    def _L1_cond_setup():
        import jax, jax.numpy as jnp
        import numpy as np
        K = 8
        T = 1.0
        D_EMBD = 128
        IN_C = 64
        OUT_C = 64
        BS = 32
        H = 1024
        HID = 128
        key = jax.random.key(seed)
        ks = jax.random.split(key, 10)
        s = lambda fan_in: 1.0 / np.sqrt(fan_in)
        return {'x': jax.random.normal(ks[0], (BS, IN_C, H), dtype=jnp.float32), 'embedding': jax.random.normal(ks[1], (BS, D_EMBD), dtype=jnp.float32), 'W0': jax.random.normal(ks[2], (D_EMBD, HID), dtype=jnp.float32) * s(D_EMBD), 'b0': jnp.zeros((HID,), dtype=jnp.float32), 'W1': jax.random.normal(ks[3], (HID, HID), dtype=jnp.float32) * s(HID), 'b1': jnp.zeros((HID,), dtype=jnp.float32), 'W2': jax.random.normal(ks[4], (HID, K), dtype=jnp.float32) * s(HID), 'b2': jnp.zeros((K,), dtype=jnp.float32), 'weight': jax.random.normal(ks[5], (K, OUT_C, IN_C, 1), dtype=jnp.float32) * s(IN_C), 'bias_k': jax.random.normal(ks[6], (K, OUT_C), dtype=jnp.float32) * 0.1}
    _L1_cond_all = _L1_cond_setup()
    _L1_cond_in = {k: v for k, v in _L1_cond_all.items() if k in ('W0', 'b0', 'W1', 'b1', 'W2', 'b2', 'weight', 'bias_k')}
    del _L1_cond_all

    def _L1_ffn_setup():
        import jax, jax.numpy as jnp
        import numpy as np
        BATCH, SEQ, D = (2, 512, 1024)
        K, TOPK, RANK = (64, 16, 16)
        ALPHA = 32.0
        SCALING = ALPHA / RANK
        key = jax.random.key(seed)
        k1, k2, k3, k4 = jax.random.split(key, 4)
        x = jax.random.normal(k1, (BATCH, SEQ, D), dtype=jnp.float32)
        A = jax.random.normal(k2, (K, RANK, D), dtype=jnp.float32) * 0.02
        B = jax.random.normal(k3, (K, D, RANK), dtype=jnp.float32) * 0.02
        Wr = jax.random.normal(k4, (K, D), dtype=jnp.float32) * 0.02
        return {'x': x, 'A': A, 'B': B, 'Wr': Wr}
    _L1_ffn_all = _L1_ffn_setup()
    _L1_ffn_in = {k: v for k, v in _L1_ffn_all.items() if k in ('A', 'B', 'Wr')}
    del _L1_ffn_all
    return {'x': x, 'cond_128': cond_128, 'fside_S_0': fside_S_0, 'L0_cond_weight': _L0_cond_in['weight'], 'L0_cond_c_weight': _L0_cond_in['c_weight'], 'L0_ffn_weight': _L0_ffn_in['weight'], 'L0_ffn_bias': _L0_ffn_in['bias'], 'L0_ffn_lora_A': _L0_ffn_in['lora_A'], 'L0_ffn_lora_B': _L0_ffn_in['lora_B'], 'L0_ffn_lora_start_indices': _L0_ffn_in['lora_start_indices'], 'L1_cond_W0': _L1_cond_in['W0'], 'L1_cond_b0': _L1_cond_in['b0'], 'L1_cond_W1': _L1_cond_in['W1'], 'L1_cond_b1': _L1_cond_in['b1'], 'L1_cond_W2': _L1_cond_in['W2'], 'L1_cond_b2': _L1_cond_in['b2'], 'L1_cond_weight': _L1_cond_in['weight'], 'L1_cond_bias_k': _L1_cond_in['bias_k'], 'L1_ffn_A': _L1_ffn_in['A'], 'L1_ffn_B': _L1_ffn_in['B'], 'L1_ffn_Wr': _L1_ffn_in['Wr']}

def reference(x, cond_128, fside_S_0, L0_cond_weight, L0_cond_c_weight, L0_ffn_weight, L0_ffn_bias, L0_ffn_lora_A, L0_ffn_lora_B, L0_ffn_lora_start_indices, L1_cond_W0, L1_cond_b0, L1_cond_W1, L1_cond_b1, L1_cond_W2, L1_cond_b2, L1_cond_weight, L1_cond_bias_k, L1_ffn_A, L1_ffn_B, L1_ffn_Wr):
    import jax
    import jax.numpy as jnp

    def _L0_cond_ref(x, c, weight, c_weight, bias):
        import jax, jax.numpy as jnp
        import numpy as np
        from jax import lax
        N, C_IN, L = (32, 64, 1024)
        C_OUT, K, GROUPS = (64, 9, 4)
        C_DIM, PAD, STRIDE = (128, 4, 1)
        out = lax.conv_general_dilated(x, weight, window_strides=(STRIDE,), padding=[(PAD, PAD)], dimension_numbers=('NCH', 'OIH', 'NCH'), feature_group_count=GROUPS)
        ctx = jnp.einsum('nd,od->no', c, c_weight)
        out = out + ctx[:, :, None] + bias[None, :, None]
        return out

    def _L0_ffn_ref(x, weight, bias, lora_A, lora_B, lora_start_indices):
        import jax, jax.numpy as jnp
        import numpy as np
        LORA_RANK = 16
        LORA_ALPHA = 16
        LORA_SCALE = LORA_ALPHA / LORA_RANK
        y = jnp.einsum('bsd,od->bso', x, weight) + bias
        B = x.shape[0]
        seg = jnp.searchsorted(lora_start_indices, jnp.arange(B), side='right') - 1
        adapter_idx = jnp.clip(seg - 1, 0, lora_A.shape[0] - 1)
        A = lora_A[adapter_idx]
        Bw = lora_B[adapter_idx]
        lo = jnp.einsum('bsr,bor->bso', jnp.einsum('bsd,brd->bsr', x, A), Bw) * LORA_SCALE
        use_lora = (seg > 0)[:, None, None]
        return y + jnp.where(use_lora, lo, jnp.zeros((), dtype=y.dtype))

    def _L1_cond_ref(x, embedding, W0, b0, W1, b1, W2, b2, weight, bias_k):
        import jax, jax.numpy as jnp
        import numpy as np
        K = 8
        T = 1.0
        D_EMBD = 128
        IN_C = 64
        OUT_C = 64
        BS = 32
        H = 1024
        HID = 128
        h = jax.nn.gelu(embedding @ W0 + b0, approximate=False)
        h = jax.nn.gelu(h @ W1 + b1, approximate=False)
        att = jax.nn.softmax((h @ W2 + b2) / T, axis=-1)
        agg_w = jnp.einsum('bk,koi->boi', att, weight[..., 0])
        agg_b = att @ bias_k
        out = jnp.einsum('boi,bih->boh', agg_w, x) + agg_b[:, :, None]
        return out

    def _L1_ffn_ref(x, A, B, Wr):
        import jax, jax.numpy as jnp
        import numpy as np
        BATCH, SEQ, D = (2, 512, 1024)
        K, TOPK, RANK = (64, 16, 16)
        ALPHA = 32.0
        SCALING = ALPHA / RANK
        prefix = x.shape[:-1]
        xf = x.reshape(-1, x.shape[-1])
        N = xf.shape[0]
        scores = xf @ Wr.T
        top_vals, top_idx = jax.lax.top_k(scores, TOPK)
        gates = jax.nn.softmax(top_vals, axis=-1)
        G = jnp.zeros((N, K), xf.dtype).at[jnp.arange(N)[:, None], top_idx].set(gates)
        h = jnp.einsum('nd,krd->nkr', xf, A)
        out = jnp.einsum('nkr,kdr->nd', h * G[:, :, None], B)
        return (out * SCALING).reshape(*prefix, -1)
    x = x + _L0_ffn_ref(_L0_cond_ref(x, cond_128, L0_cond_weight, L0_cond_c_weight, fside_S_0), L0_ffn_weight, L0_ffn_bias, L0_ffn_lora_A, L0_ffn_lora_B, L0_ffn_lora_start_indices)
    x = x + _L1_ffn_ref(_L1_cond_ref(x, cond_128, L1_cond_W0, L1_cond_b0, L1_cond_W1, L1_cond_b1, L1_cond_W2, L1_cond_b2, L1_cond_weight, L1_cond_bias_k), L1_ffn_A, L1_ffn_B, L1_ffn_Wr)
    return x

_drawn_inputs = setup_inputs


def setup_inputs(seed=0):
    import zlib

    import numpy as np

    out = dict(_drawn_inputs(seed))
    spreads = {'L1_cond_b0': (0.0, 0.8), 'L1_cond_b1': (0.0, 2.0), 'L1_cond_b2': (0.0, 2.0)}
    factors = {'L0_ffn_bias': 64.0,
     'L1_cond_W0': 4.473,
     'L1_cond_W1': 4.225,
     'L1_cond_W2': 3.989,
     'L1_cond_bias_k': 31.969}
    for name, (base, spread) in spreads.items():
        noise = np.random.default_rng([zlib.crc32(name.encode()), seed]).standard_normal(out[name].shape)
        drawn = base * np.exp(spread * noise) if base else spread * noise
        out[name] = jnp.asarray(drawn.astype(out[name].dtype))
    for name, factor in factors.items():
        out[name] = (out[name] * factor).astype(out[name].dtype)
    return out
```

```python
from contextlib import ExitStack

import concourse.bass as bass
from concourse import mybir

F32 = mybir.dt.float32
F32R = mybir.dt.float32r
I32 = mybir.dt.int32
ALU = mybir.AluOpType
ACT = mybir.ActivationFunctionType
AX_X = mybir.AxisListType.X

P = 128
NB, C, L = 32, 64, 1024
GROUPS = 4
GB = NB // GROUPS
NT = GB * C // P
TOK = NT * P
CG, CI, TAPS = 4, 16, 9
PH = 8
Q = L // PH
NCH = L // P
HALF = 512
KR_E, RANK, TOPK = 64, 16, 16
LORA = 3 * 16
LORA_LO = 64
LORA_M = LORA_LO + LORA
KC = 8
PIECES = 24
SLOTS = 3
RING = 24
ACT_STAGED, DVE_STAGED = 12, 25
NEG = -3.0e38


def adaln_ffn_kernel(nc, xp, x, wrev, pieces, lora_a, lora_b, ffn_bias, starts, cond, c_weight,
                     fside, w0, b0, w1, b1, w2, b2, mix_w, mix_b, wr, identity, pair_identity,
                     expand, batch_row, adapter_col, one_col, out):
    with ExitStack() as ctx:
        def sb(name, shape, dt=F32):
            return ctx.enter_context(nc.sbuf_tensor(name, shape, dt))

        def sem(name):
            return ctx.enter_context(nc.semaphore(name))

        raw = sb("raw", [P, SLOTS, L])
        piece_hi = sb("piece_hi", [P, SLOTS, L], F32R)
        piece_lo = sb("piece_lo", [P, SLOTS, L], F32R)
        x1 = sb("x1", [P, NT, L])
        conv_in = sb("conv_in", [P, GB, CG, Q + 1])
        u_hi = sb("u_hi", [P, NCH, TOK], F32R)
        u_lo = sb("u_lo", [P, NCH, TOK], F32R)
        v_hi = sb("v_hi", [P, NCH, TOK], F32R)
        v_lo = sb("v_lo", [P, NCH, TOK], F32R)
        ring = sb("ring", [P, SLOTS, TOK])
        toep = sb("toep", [P, 2, CG, P])
        ident = sb("ident", [P, P])
        ident2 = sb("ident2", [P, KR_E])
        ones = sb("ones", [P, P])
        cond_bc = sb("cond_bc", [P, NB, C])
        mixb_bc = sb("mixb_bc", [P, NB, C])
        agg = sb("agg", [P, NB // 2, C])
        blockdiag = sb("blockdiag", [P, NT, P])
        mixw = sb("mixw", [P, KC, C])
        expand_r = sb("expand_r", [P, L], F32R)
        lora_a_r = sb("lora_a_r", [P, PH, LORA_M], F32R)
        lora_m1 = sb("lora_m1", [P, L], F32R)
        lora_m2 = sb("lora_m2", [P, L], F32R)
        wr_r = sb("wr_r", [P, NCH, P], F32R)
        lora_h = sb("lora_h", [P, TOK])
        lora_s1 = sb("lora_s1", [P, TOK], F32R)
        lora_s2 = sb("lora_s2", [P, TOK], F32R)
        lora_mask = sb("lora_mask", [P, NB])
        score_t = sb("score_t", [P, TOK])
        top = sb("top", [P, NT, 16])
        left = sb("left", [P, 2, NT, KR_E])
        expd = sb("expd", [P, NT, KR_E])
        gate = sb("gate", [P, NT, KR_E])
        stat = sb("stat", [P, 3, NT])
        gate_r = sb("gate_r", [P, TOK], F32R)
        gate_x = sb("gate_x", [P, 2, TOK])
        starts_i = sb("starts_i", [P, 4], I32)
        starts_f = sb("starts_f", [P, 4])
        brow = sb("brow", [P, NB])
        acol = sb("acol", [P, 1])
        ecol = sb("ecol", [P, 1])
        cond_t = sb("cond_t", [P, NB])
        cw_t = sb("cw_t", [P, C])
        w2s = sb("w2s", [P, KC])
        b0s, b1s, b2s = sb("b0s", [P, 1]), sb("b1s", [P, 1]), sb("b2s", [P, KC])
        fs = sb("fs", [P, 1])
        mixb = sb("mixb", [P, C])
        hid = sb("hid", [P, 2, NB])
        ctxs = sb("ctxs", [P, 2, NB])
        att = sb("att", [NB, 4, KC])
        attstat = sb("attstat", [NB, 3])
        att_t = sb("att_t", [P, NB])
        att_pair = sb("att_pair", [P, NB // 2, KC])

        agg_part = gate_x[:, :, :].rearrange("p a (b c) -> p (a b) c", c=C)
        lora_a_raw = score_t[:, 0:PH * LORA].rearrange("p (k m) -> p k m", m=LORA)
        wr_raw = lora_h[:, :].rearrange("p (k m) -> p k m", m=KR_E)
        w0s = gate[:, 0:2, :].rearrange("p t e -> p (t e)")
        w1s = gate[:, 2:4, :].rearrange("p t e -> p (t e)")
        att_diag = expd[:, :, :].rearrange("p t e -> p (t e)").rearrange("p (b k) -> p b k", k=KC)
        reached = left[:, 0, 0:2, :].rearrange("p t e -> p (t e)").rearrange("p (n b) -> p n b", b=NB)
        count = left[:, 0, 2, :].rearrange("p (n b) -> p n b", b=NB)
        expand_stage, lora_b_stage = x1[:, 0, :], x1[:, 1, :]
        diag = x1[0:C, 2:4, :].rearrange("p t n -> p (t n)").rearrange("p (b c) -> p b c", b=NB)

        banks = [ctx.enter_context(nc.psum_tensor(f"bank{i}", [P, HALF], F32)) for i in range(8)]

        s_chain = sem("s_chain")
        s_toep = sem("s_toep")
        s_consts = sem("s_consts")
        s_lorab = sem("s_lorab")
        s_expand = sem("s_expand")
        s_ones = sem("s_ones")
        s_set_pe = sem("s_set_pe")
        s_set_act = sem("s_set_act")
        s_set_dve = sem("s_set_dve")
        s_agg = sem("s_agg")
        s_lora_ready = sem("s_lora_ready")
        s_raw = [sem(f"s_raw{i}") for i in range(SLOTS)]
        s_piece_hi = sem("s_piece_hi")
        s_piece_lo = sem("s_piece_lo")
        s_piece_used = sem("s_piece_used")
        s_convin = [sem(f"s_convin{t}") for t in range(NT)]
        s_x = sem("s_x")
        s_conv = sem("s_conv")
        s_lora_h = sem("s_lora_h")
        s_lora_masked = sem("s_lora_masked")
        s_lora_s = sem("s_lora_s")
        s_lora_lo = sem("s_lora_lo")
        s_ffn = sem("s_ffn")
        s_x1 = sem("s_x1")
        s_bd = sem("s_bd")
        s_mix = sem("s_mix")
        s_ring = sem("s_ring")
        s_hi = sem("s_hi")
        s_lo = sem("s_lo")
        s_score = sem("s_score")
        s_score_t = sem("s_score_t")
        s_score_n = sem("s_score_n")
        s_topk = sem("s_topk")
        s_exp = sem("s_exp")
        s_recip = sem("s_recip")
        s_settled = sem("s_settled")
        s_gate = sem("s_gate")
        s_gate_t = sem("s_gate_t")
        s_gate_hi = sem("s_gate_hi")
        s_gate_lo = sem("s_gate_lo")
        s_spread = sem("s_spread")
        s_gate_x = sem("s_gate_x")
        s_h = sem("s_h")
        s_out = sem("s_out")
        s_stored = sem("s_stored")

        def raw_landed(eng, g, n):
            eng.wait_ge(s_raw[n % SLOTS], g * (16 * PIECES // SLOTS) + 16 * (n // SLOTS + 1))

        def u_conv(u, b):
            return u[:, :, b * C:(b + 1) * C].rearrange("p j (g o) -> p g j o", g=CG)

        def ring_conv(item):
            return ring[:, item % SLOTS, :].rearrange("p (g j o) -> p g j o", g=CG, j=PH)

        def settled(eng):
            eng.sem_inc(s_settled, 1)

        CONV0, MIX0, H0 = 0, 8, 16
        block = ctx.enter_context(nc.Block())

        @block.sync
        def _(sp):
            def load_piece(n):
                sp.dma_start(raw[:, n % SLOTS, :], pieces[n % PIECES]).then_inc(s_raw[n % SLOTS], 16)

            def load_conv_in(g, t):
                sp.dma_start(conv_in[:, 2 * t:2 * t + 2].rearrange("p b g q -> p (b g q)"),
                             xp[bass.ds(g, 1), t].rearrange("a p n -> (a p) n")).then_inc(s_convin[t], 16)

            def load_x(g, t):
                sp.dma_start(x1[:, t, :], x[bass.ds(g, 1), t].rearrange("a p n -> (a p) n")).then_inc(s_x, 16)

            sp.dma_start(cond_t[:, :], cond).then_inc(s_chain, 16)
            sp.dma_start(w0s, w0).then_inc(s_chain, 16)
            sp.dma_start(b0s[:, :], b0).then_inc(s_chain, 16)
            for t in range(NT):
                load_conv_in(0, t)
            for n in range(SLOTS):
                load_piece(n)
            sp.wait_ge(s_ones, 2)
            for row in (0, LORA_LO):
                sp.dma_start(x1[row:row + LORA, 1, :], lora_b).then_inc(s_lorab, 16)
                sp.dma_start(x1[row + LORA:row + LORA + 1, 1, :], ffn_bias).then_inc(s_lorab, 16)
            sp.wait_ge(s_set_act, ACT_STAGED)
            sp.wait_ge(s_set_dve, DVE_STAGED)
            sp.wait_ge(s_set_pe, 9)
            for t in range(NT):
                load_x(0, t)

            def group(g, last):
                for n in range(PIECES):
                    sp.wait_ge(s_piece_lo, g * PIECES + n + 1)
                    load_piece(n + SLOTS)
                    if n == 1 and not last:
                        sp.wait_ge(s_conv, g * GB + GB)
                        for t in range(NT):
                            load_conv_in(g + 1, t)
                    if n == 21:
                        store_half(g, 0)
                store_half(g, 1)
                if not last:
                    sp.wait_ge(s_stored, g * (16 * 2 * NT) + 16 * 2 * NT)
                    for t in range(NT):
                        load_x(g + 1, t)

            def store_half(g, h):
                for t in range(NT):
                    sp.wait_ge(s_out, g * 8 + 8 + h * NT + t + 1)
                    sp.dma_start(out[bass.ds(g, 1), t, :, h * HALF:(h + 1) * HALF].rearrange("a p n -> (a p) n"),
                                 x1[:, t, h * HALF:(h + 1) * HALF]).then_inc(s_stored, 16)

            with sp.Fori(0, GROUPS - 1) as g:
                group(g, False)
            group(GROUPS - 1, True)
            sp.wait_ge(s_stored, 16 * 2 * NT * GROUPS)
            for n in range(SLOTS):
                sp.wait_ge(s_raw[n], 16 * (GROUPS * PIECES // SLOTS + 1))

        @block.gpsimd
        def _(pool):
            pool.memset(ones[:, :], 1.0).then_inc(s_ones, 1)
            pool.memset(lora_b_stage, 0.0).then_inc(s_ones, 1)
            pool.memset(lora_a_r[:, :, :].bitcast(F32), 0.0).then_inc(s_ones, 1)
            pool.memset(lora_s2[:, :].bitcast(F32), 0.0).then_inc(s_ones, 1)
            pool.wait_ge(s_ones, 4)
            pool.memset(lora_s2[96:P, :].bitcast(F32), 1.0).then_inc(s_ones, 1)
            pool.wait_ge(s_ones, 5)
            pool.memset(blockdiag[:, :, :], 0.0).then_inc(s_ones, 1)
            pool.wait_ge(s_ones, 6)
            pool.wait_ge(s_set_dve, 7)
            pool.wait_ge(s_consts, 16 * 11)
            for k in range(KC):
                weight = att_pair[:, :, k:k + 1].to_broadcast([P, NB // 2, C])
                matrix = mixw[:, k:k + 1, :].to_broadcast([P, NB // 2, C])
                if k == 0:
                    pool.tensor_tensor(agg[:, :, :], weight, matrix, ALU.mult).then_inc(s_agg, 1)
                else:
                    pool.tensor_tensor(agg_part, weight, matrix, ALU.mult).then_inc(s_agg, 1)
                    pool.wait_ge(s_agg, 2 * k)
                    pool.tensor_tensor(agg[:, :, :], agg[:, :, :], agg_part, ALU.add).then_inc(s_agg, 1)
                    pool.wait_ge(s_agg, 2 * k + 1)
            with pool.Fori(0, GROUPS) as g:
                pool.wait_ge(s_conv, g * GB + 1)
                for b in range(2):
                    rows = slice(b * C, (b + 1) * C)
                    pool.tensor_copy(blockdiag[rows, :, rows],
                                     agg[rows, bass.ds(g * NT, NT), :]).then_inc(s_bd, 1)

        @block.scalar
        def _(act):
            for p in range(PH):
                for h in range(2):
                    j = 2 * PH - 1 - PH * h - p
                    act.dma_start(toep[p * CI:(p + 1) * CI, h, :, :],
                                  wrev[:, :, j:j + PH, :].rearrange("g i j o -> i g (j o)")).then_inc(s_toep, 16)
            for to, of in ((w1s, w1), (b1s[:, :], b1), (w2s[:, :], w2), (b2s[0:1, :], b2),
                           (ident[:, :], identity), (cw_t[:, :], c_weight), (fs[0:C, :], fside)):
                act.dma_start(to, of).then_inc(s_chain, 16)
            for to, of in ((mixb[0:KC, :], mix_b), (mixw[0:C], mix_w), (mixw[C:P], mix_w),
                           (starts_i[:, :], starts.to_broadcast([P, 4])), (brow[:, :], batch_row),
                           (acol[:, :], adapter_col), (ecol[:, :], one_col),
                           (lora_a_raw, lora_a), (wr_raw, wr), (ident2[:, :], pair_identity)):
                act.dma_start(to, of).then_inc(s_consts, 16)
            act.dma_start(expand_stage, expand).then_inc(s_consts, 16)

            act.wait_ge(s_chain, 16 * 10)
            act.wait_ge(s_set_pe, 2)
            act.activation(hid[:, 0, :], banks[0][:, 0:NB], ACT.Gelu, bias=b0s[:, 0:1]).then_inc(s_set_act, 1)
            act.wait_ge(s_set_pe, 3)
            act.activation(hid[:, 1, :], banks[1][:, 0:NB], ACT.Gelu, bias=b1s[:, 0:1]).then_inc(s_set_act, 1)
            act.wait_ge(s_set_dve, 3)
            act.activation(att[:, 1, :], banks[2][0:NB, 0:KC], ACT.Exp, bias=attstat[:, 0:1],
                           accum_out=attstat[:, 1:2]).then_inc(s_set_act, 1)
            act.wait_ge(s_set_pe, 5)
            for n in range(4):
                act.activation(cond_bc[:, n * GB:(n + 1) * GB, :].rearrange("p b c -> p (b c)"), banks[4 + n][:, :],
                               ACT.Copy).then_inc(s_set_act, 1)
            act.wait_ge(s_consts, 16 * 11)
            act.wait_ge(s_lorab, 64)
            act.wait_ge(s_ones, 6)
            act.activation(lora_a_r[:, :, 0:LORA], lora_a_raw, ACT.Copy).then_inc(s_set_act, 1)
            act.activation(wr_r[:, :, 0:KR_E], wr_raw, ACT.Copy).then_inc(s_set_act, 1)
            act.activation(lora_m1[:, :], lora_b_stage, ACT.Copy).then_inc(s_set_act, 1)
            act.activation(lora_m2[0:LORA_LO, :], x1[0:LORA_LO, 1, :], ACT.Copy).then_inc(s_set_act, 1)
            act.activation(expand_r[:, :], expand_stage, ACT.Copy).then_inc(s_set_act, 1)
            act.wait_ge(s_set_pe, 9)
            for n in range(4):
                act.activation(mixb_bc[:, n * GB:(n + 1) * GB, :].rearrange("p b c -> p (b c)"), banks[4 + n][:, :],
                               ACT.Copy).then_inc(s_set_act, 1)

            def split_piece(g, n):
                raw_landed(act, g, n)
                act.activation(piece_hi[:, n % SLOTS, :], raw[:, n % SLOTS, :], ACT.Copy).then_inc(s_piece_hi, 1)

            def next_piece(g, n):
                if 8 <= n < 16:
                    act.wait_ge(s_h, g * NCH + n - 7)
                else:
                    act.wait_ge(s_piece_used, g * 16 + (n if n < 8 else n - 8) + 1)
                split_piece(g, n + SLOTS)

            def split_hi(g, item, to, of):
                act.wait_ge(s_ring, g * RING + item + 1)
                act.activation(to, of, ACT.Copy).then_inc(s_hi, 1)

            for n in range(SLOTS):
                split_piece(0, n)
            with act.Fori(0, GROUPS) as g:
                for b in range(GB):
                    split_hi(g, CONV0 + b, u_conv(u_hi, b), ring_conv(CONV0 + b))
                next_piece(g, 0)
                act.wait_ge(s_lora_masked, g + 1)
                act.activation(lora_s1[0:LORA_M, :], lora_h[0:LORA_M, :], ACT.Identity,
                               bias=ecol[0:LORA_M, 0:1]).then_inc(s_lora_s, 1)
                act.activation(lora_s2[LORA_LO:LORA_M, :], lora_h[0:LORA, :], ACT.Copy).then_inc(s_lora_s, 1)
                for n in range(1, 8):
                    next_piece(g, n)
                for c in range(NCH):
                    split_hi(g, MIX0 + c, v_hi[:, c, :], ring[:, (MIX0 + c) % SLOTS, :])
                act.wait_ge(s_score, g + 1)
                act.activation(score_t[:, :], banks[4][:, :], ACT.Copy).then_inc(s_score_t, 1)
                next_piece(g, 8)
                act.wait_ge(s_topk, 7 * g + 3)
                for t in range(NT):
                    act.activation(expd[:, t, :], left[:, 1, t, :], ACT.Exp,
                                   bias=stat[:, 0, t:t + 1]).then_inc(s_exp, 1)
                next_piece(g, 9)
                act.wait_ge(s_gate_t, g + 1)
                act.activation(gate_r[0:KR_E, :], banks[6][0:KR_E, :], ACT.Copy).then_inc(s_gate_hi, 1)
                next_piece(g, 10)

                def spread(c):
                    act.wait_ge(s_spread, g * NCH + c + 1)
                    if c >= 2:
                        act.wait_ge(s_ring, g * RING + H0 + c - 1)
                    act.activation(gate_x[:, c % 2, :], banks[(7, 5)[c % 2]][:, :], ACT.Copy).then_inc(s_gate_x, 1)

                for c in range(0, NCH, 2):
                    spread(c)
                    spread(c + 1)
                    for k in (c, c + 1):
                        split_hi(g, H0 + k, u_hi[:, k, :], ring[:, (H0 + k) % SLOTS, :])
                        if k != c or c == NCH - 2:
                            next_piece(g, 11 + c // 2 + (k == NCH - 1))
                for n in range(16, PIECES):
                    next_piece(g, n)

        @block.vector
        def _(dve):
            def wait_self(n):
                dve.wait_ge(s_set_dve, n)

            dve.wait_ge(s_ones, 6)
            dve.sem_inc(s_out, 8)
            dve.wait_ge(s_chain, 16 * 10)
            dve.wait_ge(s_set_pe, 1)
            dve.tensor_scalar(ctxs[0:C, 0, :], banks[3][0:C, 0:NB], fs[0:C, 0:1], None, ALU.add).then_inc(s_set_dve, 1)
            wait_self(1)
            dve.tensor_tensor(diag, ident[0:C, None, 0:C].to_broadcast([C, NB, C]),
                              ctxs[0:C, 0, :, None].to_broadcast([C, NB, C]), ALU.mult).then_inc(s_set_dve, 1)
            dve.wait_ge(s_set_pe, 4)
            dve.tensor_reduce(attstat[:, 0:1], banks[2][0:NB, 0:KC], AX_X, ALU.max, negate=True).then_inc(s_set_dve, 1)
            dve.wait_ge(s_set_act, 3)
            dve.reciprocal(attstat[:, 2:3], attstat[:, 1:2]).then_inc(s_set_dve, 1)
            wait_self(4)
            dve.tensor_scalar(att[:, 2, :], att[:, 1, :], attstat[:, 2:3], None, ALU.mult).then_inc(s_set_dve, 1)
            wait_self(5)
            dve.tensor_tensor(att_diag[0:NB], ident[0:NB, 0:NB, None].to_broadcast([NB, NB, KC]),
                              att[:, 2, None, :].to_broadcast([NB, NB, KC]), ALU.mult).then_inc(s_set_dve, 1)
            dve.wait_ge(s_set_pe, 7)
            both = banks[1][:, 0:NB * KC].rearrange("p (t b k) -> p t b k", b=2, k=KC)
            dve.tensor_copy(att_pair[0:C], both[0:C, :, 0, :])
            dve.tensor_copy(att_pair[C:P], both[C:P, :, 1, :]).then_inc(s_set_dve, 1)
            dve.tensor_copy(att_t[0:KC, :], banks[3][0:KC, 0:NB]).then_inc(s_set_dve, 1)
            dve.wait_ge(s_set_pe, 8)
            dve.tensor_copy(ctxs[0:C, 1, :], banks[0][0:C, 0:NB]).then_inc(s_set_dve, 1)
            wait_self(9)
            dve.tensor_tensor(diag, ident[0:C, None, 0:C].to_broadcast([C, NB, C]),
                              ctxs[0:C, 1, :, None].to_broadcast([C, NB, C]), ALU.mult).then_inc(s_set_dve, 1)
            dve.wait_ge(s_consts, 16 * 11)
            dve.tensor_copy(starts_f[:, :], starts_i[:, :]).then_inc(s_set_dve, 1)
            wait_self(11)
            for n in range(4):
                dve.tensor_scalar(reached[:, n, :], brow[:, :], starts_f[:, n:n + 1], None,
                                  ALU.is_ge).then_inc(s_set_dve, 1)
            wait_self(15)
            low, high = count[:, 0, :], count[:, 1, :]
            dve.tensor_scalar(low, reached[:, 0, :], -1.0, 2.0, ALU.mult, ALU.add).then_inc(s_set_dve, 1)
            wait_self(16)
            dve.tensor_tensor(low, low, reached[:, 1, :], ALU.mult).then_inc(s_set_dve, 1)
            wait_self(17)
            dve.tensor_tensor(low, low, reached[:, 0, :], ALU.add).then_inc(s_set_dve, 1)
            wait_self(18)
            dve.scalar_tensor_tensor(out=high, in0=reached[:, 3, :], scalar=3.0, in1=low,
                                     op0=ALU.add, op1=ALU.subtract).then_inc(s_set_dve, 1)
            wait_self(19)
            dve.tensor_tensor(high, high, reached[:, 2, :], ALU.mult).then_inc(s_set_dve, 1)
            wait_self(20)
            dve.tensor_tensor(high, high, low, ALU.add).then_inc(s_set_dve, 1)
            wait_self(21)
            dve.tensor_scalar(lora_mask[:, :], high, 2.0, acol[:, 0:1], ALU.subtract, ALU.is_equal).then_inc(s_set_dve, 1)
            dve.wait_ge(s_set_act, 12)
            dve.tensor_tensor(lora_a_r[:, :, LORA_LO:LORA_M], lora_a_raw,
                              lora_a_r[:, :, 0:LORA].bitcast(F32), ALU.subtract).then_inc(s_set_dve, 1)
            dve.tensor_tensor(wr_r[:, :, KR_E:P], wr_raw, wr_r[:, :, 0:KR_E].bitcast(F32),
                              ALU.subtract).then_inc(s_set_dve, 1)
            dve.tensor_tensor(lora_m2[LORA_LO:P, :], x1[LORA_LO:P, 1, :], lora_m1[LORA_LO:P, :].bitcast(F32),
                              ALU.subtract).then_inc(s_set_dve, 1)

            def split_piece(g, n):
                dve.wait_ge(s_piece_hi, g * PIECES + n + 1)
                dve.tensor_tensor(piece_lo[:, n % SLOTS, :], raw[:, n % SLOTS, :],
                                  piece_hi[:, n % SLOTS, :].bitcast(F32), ALU.subtract).then_inc(s_piece_lo, 1)

            def ring_free(g, item):
                if isinstance(g, int) and g * RING + item < SLOTS:
                    return
                dve.wait_ge(s_lo, g * RING + item - SLOTS + 1 + SLOTS)

            def split_lo(g, item, to, of, hi):
                dve.wait_ge(s_hi, g * RING + item + 1)
                dve.tensor_tensor(to, of, hi, ALU.subtract).then_inc(s_lo, 1)

            dve.sem_inc(s_lo, SLOTS)
            for n in range(SLOTS):
                split_piece(0, n)
            dve.wait_ge(s_set_act, 16)
            with dve.Fori(0, GROUPS) as g:
                def conv_lo(b):
                    split_lo(g, CONV0 + b, u_conv(u_lo, b), ring_conv(CONV0 + b), u_conv(u_hi, b).bitcast(F32))

                for b in range(GB):
                    dve.wait_ge(s_conv, g * GB + b + 1)
                    ring_free(g, CONV0 + b)
                    bias = cond_bc[:, bass.ds(g * GB + b, 1), :].rearrange("p a (g o) -> p (a g) o", g=CG)
                    dve.tensor_tensor(ring_conv(CONV0 + b),
                                      banks[4 + b % 4][:, :].rearrange("p (g j o) -> p g j o", g=CG, j=PH),
                                      bias[:, :, None, :].to_broadcast([P, CG, PH, CI]), ALU.add).then_inc(s_ring, 1)
                    if b:
                        conv_lo(b - 1)
                conv_lo(GB - 1)
                split_piece(g, SLOTS)
                dve.wait_ge(s_lora_h, g + 1)
                mask = lora_mask[0:LORA_M, bass.ds(g * GB, GB)]
                dve.tensor_tensor(lora_h[0:LORA_M, :].rearrange("p (b c) -> p b c", b=GB),
                                  banks[4][0:LORA_M, :].rearrange("p (b c) -> p b c", b=GB),
                                  mask[:, :, None].to_broadcast([LORA_M, GB, C]), ALU.mult).then_inc(s_lora_masked, 1)
                dve.wait_ge(s_lora_s, 2 * g + 1)
                dve.wait_ge(s_lora_masked, g + 1)
                dve.tensor_tensor(lora_s2[0:LORA, :], lora_h[0:LORA, :], lora_s1[0:LORA, :].bitcast(F32),
                                  ALU.subtract).then_inc(s_lora_lo, 1)
                split_piece(g, 4)
                split_piece(g, 5)
                dve.wait_ge(s_x, g * (16 * NT) + 16 * NT)
                for h in range(2):
                    dve.wait_ge(s_ffn, g * 2 + h + 1)
                    for t in range(NT):
                        half = x1[:, t, h * HALF:(h + 1) * HALF]
                        dve.tensor_tensor(half, half, banks[4 * h + t][:, :], ALU.add).then_inc(s_x1, 1)
                    for n in ((6, 7, 8, 9), (10,))[h]:
                        split_piece(g, n)

                def mix_lo(c):
                    split_lo(g, MIX0 + c, v_lo[:, c, :], ring[:, (MIX0 + c) % SLOTS, :], v_hi[:, c, :].bitcast(F32))

                for c in range(NCH):
                    dve.wait_ge(s_mix, g * NCH + c + 1)
                    ring_free(g, MIX0 + c)
                    bias = mixb_bc[:, bass.ds(g * GB, GB), :].rearrange("p b c -> p (b c)")
                    dve.tensor_tensor(ring[:, (MIX0 + c) % SLOTS, :], banks[c % 4][:, :], bias,
                                      ALU.add).then_inc(s_ring, 1)
                    if c:
                        mix_lo(c - 1)
                mix_lo(NCH - 1)
                dve.wait_ge(s_score_n, g + 1)
                scores = left[:, 1, :, :]
                dve.tensor_copy(scores.rearrange("p t e -> p (t e)"), banks[5][:, 0:NT * KR_E]).then_inc(s_topk, 1)
                dve.wait_ge(s_topk, 7 * g + 1)
                settled(dve)
                for t in range(NT):
                    last = dve.max(top[:, t, 0:8], scores[:, t, :])
                last.then_inc(s_topk, 1)
                dve.wait_ge(s_topk, 7 * g + 2)
                dve.tensor_scalar(stat[:, 0, :], top[:, :, 0:1].rearrange("p t a -> p (t a)"), -1.0, None,
                                  ALU.mult).then_inc(s_topk, 1)
                settled(dve)
                for t in range(NT):
                    last = dve.match_replace(left[:, 0, t, :], top[:, t, 0:8], scores[:, t, :], NEG)
                last.then_inc(s_topk, 1)
                dve.wait_ge(s_topk, 7 * g + 4)
                settled(dve)
                for t in range(NT):
                    last = dve.max(top[:, t, 8:16], left[:, 0, t, :])
                last.then_inc(s_topk, 1)
                dve.wait_ge(s_exp, g * NT + NT)
                settled(dve)
                dve.wait_ge(s_topk, 7 * g + 5)
                settled(dve)
                for t in range(NT):
                    last = dve.match_replace(left[:, 1, t, :], top[:, t, 8:16], left[:, 0, t, :], NEG)
                last.then_inc(s_topk, 1)
                dve.wait_ge(s_topk, 7 * g + 6)
                for t in range(NT):
                    last = dve.scalar_tensor_tensor(out=expd[:, t, :], in0=left[:, 1, t, :], scalar=NEG,
                                                    in1=expd[:, t, :], op0=ALU.is_equal, op1=ALU.mult,
                                                    accum_out=stat[:, 1, t:t + 1])
                last.then_inc(s_topk, 1)
                dve.wait_ge(s_topk, 7 * g + 7)
                dve.reciprocal(stat[:, 2, :], stat[:, 1, :]).then_inc(s_recip, 1)
                dve.wait_ge(s_recip, g + 1)
                for t in range(NT):
                    dve.tensor_scalar(gate[:, t, :], expd[:, t, :], stat[:, 2, t:t + 1], 2.0, ALU.mult,
                                      ALU.mult).then_inc(s_gate, 1)
                split_piece(g, 11)
                split_piece(g, 12)
                dve.wait_ge(s_gate_t, g + 1)
                dve.wait_ge(s_gate_hi, g + 1)
                dve.tensor_tensor(gate_r[KR_E:P, :], banks[6][0:KR_E, :], gate_r[0:KR_E, :].bitcast(F32),
                                  ALU.subtract).then_inc(s_gate_lo, 1)
                split_piece(g, 13)

                def gated(c):
                    dve.wait_ge(s_h, g * NCH + c + 1)
                    dve.wait_ge(s_gate_x, g * NCH + c + 1)
                    ring_free(g, H0 + c)
                    dve.tensor_tensor(ring[:, (H0 + c) % SLOTS, :], banks[c % 4][:, :], gate_x[:, c % 2, :],
                                      ALU.mult).then_inc(s_ring, 1)

                for c in range(0, NCH, 2):
                    for k in (c, c + 1):
                        if c < NCH - 2:
                            gated(k)
                    for k in (c, c + 1):
                        if c == NCH - 2:
                            gated(k)
                        split_lo(g, H0 + k, u_lo[:, k, :], ring[:, (H0 + k) % SLOTS, :], u_hi[:, k, :].bitcast(F32))
                        if k != c or c == NCH - 2:
                            split_piece(g, 14 + c // 2 + (k == NCH - 1))
                for h in range(2):
                    for n in ((19, 20, 21), (22, 23, 24, 25))[h]:
                        split_piece(g, n)
                    dve.wait_ge(s_piece_used, g * 16 + 8 + 4 * h + 4)
                    for t in range(NT):
                        half = x1[:, t, h * HALF:(h + 1) * HALF]
                        dve.tensor_tensor(half, half, banks[4 - 4 * h + t][:, :], ALU.add).then_inc(s_out, 1)
                split_piece(g, 26)

        @block.tensor
        def _(pe):
            pe.wait_ge(s_chain, 16 * 10)
            pe.matmul(banks[3][0:C, 0:NB], cw_t[:, :], cond_t[:, :], start=True, stop=True).then_inc(s_set_pe, 1)
            pe.matmul(banks[0][:, 0:NB], w0s, cond_t[:, :], start=True, stop=True).then_inc(s_set_pe, 1)
            pe.wait_ge(s_set_act, 1)
            pe.matmul(banks[1][:, 0:NB], w1s, hid[:, 0, :], start=True, stop=True).then_inc(s_set_pe, 1)
            pe.wait_ge(s_ones, 1)
            pe.wait_ge(s_set_act, 2)
            pe.matmul(banks[2][0:NB, 0:KC], hid[:, 1, :], w2s[:, :], start=True, stop=False)
            pe.matmul(banks[2][0:NB, 0:KC], ones[0:1, 0:NB], b2s[0:1, :], start=False, stop=True).then_inc(s_set_pe, 1)

            def spread_diag():
                for n in range(4):
                    mm = pe.matmul(banks[4 + n][:, :], ones[0:C, :],
                                   diag[:, n * GB:(n + 1) * GB, :].rearrange("p b c -> p (b c)"), start=True, stop=True)
                mm.then_inc(s_set_pe, 1)

            pe.wait_ge(s_set_dve, 2)
            spread_diag()
            pe.wait_ge(s_set_dve, 5)
            pe.transpose(banks[3][0:KC, 0:NB], att[:, 2, :], ident[0:NB, 0:NB]).then_inc(s_set_pe, 1)
            pe.wait_ge(s_set_dve, 6)
            pe.matmul(banks[1][:, 0:NB * KC], ones[0:NB, :], att_diag[0:NB].rearrange("p b k -> p (b k)"),
                      start=True, stop=True).then_inc(s_set_pe, 1)
            pe.wait_ge(s_consts, 16 * 11)
            pe.wait_ge(s_set_dve, 8)
            pe.matmul(banks[0][0:C, 0:NB], mixb[0:KC, :], att_t[0:KC, :], start=True, stop=True).then_inc(s_set_pe, 1)
            pe.wait_ge(s_set_dve, 10)
            pe.wait_ge(s_set_act, 7)
            spread_diag()
            pe.wait_ge(s_toep, 16 * 2 * PH)
            pe.wait_ge(s_set_act, 16)
            pe.wait_ge(s_set_dve, 25)

            def product(to, left_hi, left_lo, right_hi, right_lo, first, last):
                pe.matmul(to, left_hi, right_hi, start=first, stop=False)
                pe.matmul(to, left_hi, right_lo, start=False, stop=False)
                return pe.matmul(to, left_lo, right_hi, start=False, stop=last)

            def piece_ready(g, n):
                pe.wait_ge(s_piece_lo, g * PIECES + n + 1)

            def split_done(g, item):
                pe.wait_ge(s_lo, g * RING + item + 1 + SLOTS)

            def columns_piece(n, c):
                return (piece_hi[:, n % SLOTS, c * HALF:(c + 1) * HALF], piece_lo[:, n % SLOTS, c * HALF:(c + 1) * HALF])

            with pe.Fori(0, GROUPS) as g:
                for b in range(GB):
                    if b % 2 == 0:
                        pe.wait_ge(s_convin[b // 2], g * 16 + 16)
                    if b < 4:
                        pe.wait_ge(s_out, g * 8 + b + 1)
                    else:
                        pe.wait_ge(s_ring, g * RING + CONV0 + b - 3)
                    for cg in range(CG):
                        for h in range(2):
                            mm = pe.matmul(banks[4 + b % 4][:, cg * P:(cg + 1) * P], conv_in[:, b, cg, h:h + Q],
                                           toep[:, h, cg, :], start=(h == 0), stop=(h == 1))
                    mm.then_inc(s_conv, 1)

                def ffn_piece(n):
                    h, j = n // 4, n % 4
                    piece_ready(g, n)
                    for t in range(NT):
                        if n == 0:
                            pe.wait_ge(s_out, g * 8 + 4 + t + 1)
                            split_done(g, CONV0 + 2 * t + 1)
                        for c in range(2):
                            k = 2 * j + c
                            mm = product(banks[4 * h + t][:, :], u_hi[:, k, t * P:(t + 1) * P],
                                         u_lo[:, k, t * P:(t + 1) * P], *columns_piece(n, c), k == 0, False)
                    mm.then_inc(s_piece_used, 1)

                def lora_second(h):
                    pe.wait_ge(s_lora_s, 2 * g + 2)
                    pe.wait_ge(s_lora_lo, g + 1)
                    for t in range(NT):
                        pe.matmul(banks[4 * h + t][:, :], lora_s1[0:LORA_M, t * P:(t + 1) * P],
                                  lora_m1[0:LORA_M, h * HALF:(h + 1) * HALF], start=False, stop=False)
                        mm = pe.matmul(banks[4 * h + t][:, :], lora_s2[0:LORA_M + 1, t * P:(t + 1) * P],
                                       lora_m2[0:LORA_M + 1, h * HALF:(h + 1) * HALF], start=False, stop=True)
                    mm.then_inc(s_ffn, 1)

                ffn_piece(0)
                for k in range(NCH):
                    for part in (u_hi, u_lo):
                        mm = pe.matmul(banks[4][0:LORA_M, :], lora_a_r[:, k, :], part[:, k, :],
                                       start=(k == 0 and part is u_hi), stop=(k == NCH - 1 and part is u_lo))
                mm.then_inc(s_lora_h, 1)
                for n in (1, 2, 3):
                    ffn_piece(n)
                lora_second(0)
                pe.wait_ge(s_lora_masked, g + 1)
                for n in (4, 5, 6, 7):
                    ffn_piece(n)
                lora_second(1)

                def mix(c):
                    if c == 0:
                        pe.wait_ge(s_bd, 2 * g + 2)
                        pe.wait_ge(s_x1, g * 8 + 4)
                    if c == 4:
                        pe.wait_ge(s_x1, g * 8 + 8)
                    if c >= 4:
                        pe.wait_ge(s_ring, g * RING + MIX0 + c - 3)
                    for t in range(NT):
                        mm = pe.matmul(banks[c % 4][:, t * P:(t + 1) * P], x1[:, t, c * P:(c + 1) * P],
                                       blockdiag[:, t, :], start=True, stop=True)
                    mm.then_inc(s_mix, 1)

                def score(c):
                    split_done(g, MIX0 + c)
                    if c == 0:
                        pe.wait_ge(s_x1, g * 8 + 5)
                    pe.matmul(banks[4][:, :], wr_r[:, c, :], v_hi[:, c, :], start=(c == 0), stop=False)
                    mm = pe.matmul(banks[4][:, :], wr_r[:, c, :], v_lo[:, c, :], start=False, stop=(c == NCH - 1))
                    if c == NCH - 1:
                        mm.then_inc(s_score, 1)

                for c in range(NCH):
                    mix(c)
                    if c >= 2:
                        score(c - 2)

                def h_part(c, ks):
                    n = 8 + c
                    if ks[0] == 0:
                        piece_ready(g, n)
                        if c >= 4:
                            pe.wait_ge(s_ring, g * RING + H0 + c - 3)
                    for k in ks:
                        if c == 0:
                            split_done(g, MIX0 + k)
                        if c == 0 and k == 0:
                            pe.wait_ge(s_ring, g * RING + MIX0 + 8)
                        cols = slice(k * P, (k + 1) * P)
                        mm = product(banks[c % 4][:, :], piece_hi[:, n % SLOTS, cols], piece_lo[:, n % SLOTS, cols],
                                     v_hi[:, k, :], v_lo[:, k, :], k == 0, k == NCH - 1)
                    if ks[-1] == NCH - 1:
                        mm.then_inc(s_h, 1)

                def spread(c):
                    if c == 0:
                        pe.wait_ge(s_gate_hi, g + 1)
                        pe.wait_ge(s_gate_lo, g + 1)
                    if c >= 2:
                        pe.wait_ge(s_gate_x, g * NCH + c - 1)
                    pe.matmul(banks[(7, 5)[c % 2]][:, :], expand_r[:, c * P:(c + 1) * P], gate_r[:, :],
                              start=True, stop=True).then_inc(s_spread, 1)

                first, second = (0, 1, 2, 3), (4, 5, 6, 7)
                h_part(0, first)
                score(6)
                score(7)
                h_part(0, second)
                pe.wait_ge(s_score_t, g + 1)
                for t in range(NT):
                    mm = pe.matmul(banks[5][:, t * KR_E:(t + 1) * KR_E], score_t[:, t * P:(t + 1) * P],
                                   ident2[:, :], start=True, stop=True)
                mm.then_inc(s_score_n, 1)
                h_part(1, first + second)
                h_part(2, first + second)
                for t in range(NT):
                    pe.wait_ge(s_gate, g * NT + t + 1)
                    settled(pe)
                    mm = pe.transpose(banks[6][0:KR_E, t * P:(t + 1) * P], gate[:, t, :], ident[:, :])
                mm.then_inc(s_gate_t, 1)
                for c in range(3, NCH):
                    h_part(c, first)
                    if c < 7:
                        spread(2 * (c - 3))
                        spread(2 * (c - 3) + 1)
                    h_part(c, second)

                for n in range(16, PIECES):
                    h, j = (n - 16) // 4, n % 4
                    piece_ready(g, n)
                    if n == 16:
                        pe.wait_ge(s_gate_x, g * NCH + NCH)
                    for c in range(2):
                        k = 2 * j + c
                        if h == 0:
                            split_done(g, H0 + k)
                        for t in range(NT):
                            mm = product(banks[4 - 4 * h + t][:, :], u_hi[:, k, t * P:(t + 1) * P],
                                         u_lo[:, k, t * P:(t + 1) * P], *columns_piece(n, c), k == 0, k == NCH - 1)
                    mm.then_inc(s_piece_used, 1)


def kernel(x, cond_128, fside_S_0, L0_cond_weight, L0_cond_c_weight, L0_ffn_weight, L0_ffn_bias,
           L0_ffn_lora_A, L0_ffn_lora_B, L0_ffn_lora_start_indices, L1_cond_W0, L1_cond_b0, L1_cond_W1,
           L1_cond_b1, L1_cond_W2, L1_cond_b2, L1_cond_weight, L1_cond_bias_k, L1_ffn_A, L1_ffn_B, L1_ffn_Wr):
    import numpy as np
    import concourse.bacc as bacc
    from concourse.bass_utils import run_bass_kernel_spmd

    x = np.asarray(x)
    padded = np.pad(x, ((0, 0), (0, 0), (TAPS // 2, TAPS // 2)))
    xp = padded.reshape(GROUPS, NT, 2, CG, CI, Q + 1, PH).transpose(0, 1, 6, 4, 2, 3, 5)
    taps = np.asarray(L0_cond_weight).reshape(CG, CI, CI, TAPS).transpose(0, 2, 3, 1)[:, :, ::-1, :]
    wrev = np.pad(taps, ((0, 0), (0, 0), (PH - 1, PH - 1), (0, 0)))
    w = np.asarray(L0_ffn_weight).reshape(2, HALF, Q, 4, 2).transpose(0, 3, 2, 4, 1).reshape(8, P, L)
    a = np.asarray(L1_ffn_A).reshape(NCH, P, NCH, P).transpose(0, 3, 2, 1).reshape(8, P, L)
    b = (np.asarray(L1_ffn_B).transpose(0, 2, 1).reshape(4, 2, P, 2, HALF)
         .transpose(3, 0, 2, 1, 4).reshape(8, P, L))
    eye = np.eye(P, dtype=np.float32)
    rows = np.arange(P)
    adapter = (rows % LORA_LO) // RANK
    arrays = {
        "xp": xp.reshape(GROUPS, NT, P, 2 * CG * (Q + 1)),
        "x": x.reshape(GROUPS, NT, P, L),
        "wrev": wrev,
        "pieces": np.concatenate([w, a, b]),
        "lora_a": np.asarray(L0_ffn_lora_A).reshape(LORA, Q, PH).transpose(1, 2, 0),
        "lora_b": np.asarray(L0_ffn_lora_B).transpose(0, 2, 1).reshape(LORA, L),
        "ffn_bias": np.asarray(L0_ffn_bias).reshape(1, L),
        "starts": np.asarray(L0_ffn_lora_start_indices).reshape(1, 4),
        "cond": np.asarray(cond_128).T,
        "c_weight": np.asarray(L0_cond_c_weight).T,
        "fside": np.asarray(fside_S_0).reshape(C, 1),
        "w0": np.asarray(L1_cond_W0), "b0": np.asarray(L1_cond_b0).reshape(P, 1),
        "w1": np.asarray(L1_cond_W1), "b1": np.asarray(L1_cond_b1).reshape(P, 1),
        "w2": np.asarray(L1_cond_W2), "b2": np.asarray(L1_cond_b2).reshape(1, KC),
        "mix_w": np.asarray(L1_cond_weight).reshape(KC, C, C).transpose(2, 0, 1),
        "mix_b": np.asarray(L1_cond_bias_k),
        "wr": np.asarray(L1_ffn_Wr).reshape(KR_E, NCH, P).transpose(2, 1, 0),
        "identity": eye,
        "pair_identity": np.concatenate([eye[:C, :C], eye[:C, :C]]),
        "expand": np.tile(np.repeat(np.eye(KR_E, dtype=np.float32), RANK, axis=1), (2, 1)),
        "batch_row": np.tile(np.arange(NB, dtype=np.float32), (P, 1)),
        "adapter_col": adapter.astype(np.float32).reshape(P, 1),
        "one_col": (rows == LORA).astype(np.float32).reshape(P, 1),
    }
    nc = bacc.Bacc("TRN2", target_bir_lowering=False, num_devices=1)
    aps = {}
    for name, v in arrays.items():
        arrays[name] = v = np.ascontiguousarray(v)
        aps[name] = nc.dram_tensor(name, v.shape, mybir.dt.from_np(v.dtype), kind="ExternalInput").ap()
    out = nc.dram_tensor("out", (GROUPS, NT, P, L), F32, kind="ExternalOutput").ap()
    adaln_ffn_kernel(nc, **aps, out=out)
    result = run_bass_kernel_spmd(nc, [arrays], core_ids=[0]).results[0]["out"]
    return result.reshape(NB, C, L)
```

```python
from contextlib import ExitStack

import concourse.bass as bass
from concourse import mybir

F32 = mybir.dt.float32
F32R = mybir.dt.float32r
I32 = mybir.dt.int32
ALU = mybir.AluOpType
ACT = mybir.ActivationFunctionType
AX_X = mybir.AxisListType.X

P = 128
NB, C, L = 32, 64, 1024
GROUPS = 4
GB = NB // GROUPS
NT = GB * C // P
TOK = NT * P
CG, CI, TAPS = 4, 16, 9
PH = 8
Q = L // PH
NCH = L // P
HALF = 512
KR_E, RANK, TOPK = 64, 16, 16
LORA = 3 * 16
FIRST = (("ident", 128), ("cond", 32), ("c_weight", 64), ("fside", 1), ("b0", 1), ("b1", 1), ("w2", 8), ("b2", 8))
LATER = (("mix_b", 64), ("batch_row", 32), ("adapter", 1), ("one", 1), ("mix_w", 512))
LORA_LO = 64
LORA_M = LORA_LO + LORA
KC = 8
PIECES = 24
SLOTS = 3
RING = 24
LAG = 3
NEG = -3.0e38


def adaln_ffn_kernel(nc, conv_x, x, taps, pieces, first_consts, hidden_w, later_consts, lora_a, lora_b,
                     starts, wr, expand, out):
    with ExitStack() as ctx:
        def sb(name, shape, dt=F32):
            return ctx.enter_context(nc.sbuf_tensor(name, shape, dt))

        def sem(name):
            return ctx.enter_context(nc.semaphore(name))

        raw = sb("raw", [P, SLOTS, L])
        piece_hi = sb("piece_hi", [P, SLOTS, L], F32R)
        piece_lo = sb("piece_lo", [P, SLOTS, L], F32R)
        x1 = sb("x1", [P, NT, L])
        conv_in = sb("conv_in", [P, GB, CG, Q + 1])
        u_hi = sb("u_hi", [P, NCH, TOK], F32R)
        u_lo = sb("u_lo", [P, NCH, TOK], F32R)
        v_hi = sb("v_hi", [P, NCH, TOK], F32R)
        v_lo = sb("v_lo", [P, NCH, TOK], F32R)
        ring = sb("ring", [P, SLOTS, TOK])
        toep = sb("toep", [P, CG, 2, P])
        ones = sb("ones", [P, P])
        cond_bc = sb("cond_bc", [P, NB, C])
        mixb_bc = sb("mixb_bc", [P, NB, C])
        agg = sb("agg", [P, NB // 2, C])
        blockdiag = sb("blockdiag", [P, NT, P])
        expand_r = sb("expand_r", [P, L], F32R)
        lora_a_r = sb("lora_a_r", [P, PH, LORA_M], F32R)
        lora_m1 = sb("lora_m1", [P, L], F32R)
        lora_m2 = sb("lora_m2", [P, L], F32R)
        wr_r = sb("wr_r", [P, NCH, P], F32R)
        lora_h = sb("lora_h", [P, TOK])
        lora_s1 = sb("lora_s1", [P, TOK], F32R)
        lora_s2 = sb("lora_s2", [P, TOK], F32R)
        lora_mask = sb("lora_mask", [P, NB])
        score_t = sb("score_t", [P, TOK])
        top = sb("top", [P, NT, 16])
        left = sb("left", [P, 2, NT, KR_E])
        expd = sb("expd", [P, NT, KR_E])
        gate = sb("gate", [P, NT, KR_E])
        stat = sb("stat", [P, 3, NT])
        gate_r = sb("gate_r", [P, TOK], F32R)
        gate_x = sb("gate_x", [P, 2, TOK])
        consts1 = sb("consts1", [P, sum(w for _, w in FIRST)])
        consts2 = sb("consts2", [P, sum(w for _, w in LATER)])
        starts_i = sb("starts_i", [P, 4], I32)
        starts_f = sb("starts_f", [P, 4])
        hid = sb("hid", [P, 2, NB])
        ctxs = sb("ctxs", [P, 2, NB])
        att = sb("att", [NB, 3, KC])
        attstat = sb("attstat", [NB, 3])
        att_t = sb("att_t", [P, NB])
        att_pair = sb("att_pair", [P, NB // 2, KC])

        def columns(tile, names, name):
            at = 0
            for n, w in names:
                if n == name:
                    return tile[:, at:at + w]
                at += w

        ident, cond_t, cw_t, fs, b0s, b1s, w2s, b2s = (columns(consts1, FIRST, n) for n, _ in FIRST)
        mixb, brow, acol, ecol, mixw = (columns(consts2, LATER, n) for n, _ in LATER)
        mixw = mixw.rearrange("p (k c) -> p k c", c=C)
        agg_part = gate_x[:, :, :].rearrange("p a (b c) -> p (a b) c", c=C)
        lora_a_raw = score_t[:, 0:PH * LORA].rearrange("p (k m) -> p k m", m=LORA)
        wr_raw = blockdiag[:, :, :].rearrange("p t n -> p (t n)").rearrange("p (k m) -> p k m", m=KR_E)
        w0s = gate[:, 0:2, :].rearrange("p t e -> p (t e)")
        w1s = gate[:, 2:4, :].rearrange("p t e -> p (t e)")
        hidden_stage = gate[:, :, :].rearrange("p t e -> p (t e)")
        att_diag = expd[:, :, :].rearrange("p t e -> p (t e)").rearrange("p (b k) -> p b k", k=KC)
        reached = left[:, 0, 0:2, :].rearrange("p t e -> p (t e)").rearrange("p (n b) -> p n b", b=NB)
        count = left[:, 0, 2, :].rearrange("p (n b) -> p n b", b=NB)
        expand_stage, lora_b_stage = x1[:, 0, :], x1[:, 1, :]
        diag = x1[0:C, 2:4, :].rearrange("p t n -> p (t n)").rearrange("p (b c) -> p b c", b=NB)

        banks = [ctx.enter_context(nc.psum_tensor(f"bank{i}", [P, HALF], F32)) for i in range(8)]

        s_first = sem("s_first")
        s_taps = sem("s_taps")
        s_later = sem("s_later")
        s_starts = sem("s_starts")
        s_expand = sem("s_expand")
        s_ones = sem("s_ones")
        s_p_ctx = sem("s_p_ctx")
        s_p_hid = sem("s_p_hid")
        s_p_logit = sem("s_p_logit")
        s_p_ctx_bc = sem("s_p_ctx_bc")
        s_p_att = sem("s_p_att")
        s_p_mixb_bc = sem("s_p_mixb_bc")
        s_hid = sem("s_hid")
        s_att_exp = sem("s_att_exp")
        s_ctx_bc = sem("s_ctx_bc")
        s_mixb_bc = sem("s_mixb_bc")
        s_const_hi = sem("s_const_hi")
        s_ctx = sem("s_ctx")
        s_att = sem("s_att")
        s_mixb = sem("s_mixb")
        s_adapter = sem("s_adapter")
        s_const_lo = sem("s_const_lo")
        s_agg = sem("s_agg")
        s_raw = [sem(f"s_raw{i}") for i in range(SLOTS)]
        s_piece_hi = sem("s_piece_hi")
        s_piece_lo = sem("s_piece_lo")
        s_piece_used = sem("s_piece_used")
        s_convin = [sem(f"s_convin{t}") for t in range(NT)]
        s_x = sem("s_x")
        s_conv = sem("s_conv")
        s_lora_h = sem("s_lora_h")
        s_lora_masked = sem("s_lora_masked")
        s_lora_s = sem("s_lora_s")
        s_lora_lo = sem("s_lora_lo")
        s_ffn = sem("s_ffn")
        s_fin = sem("s_fin")
        s_x1 = sem("s_x1")
        s_bd = sem("s_bd")
        s_mix = sem("s_mix")
        s_ring = sem("s_ring")
        s_hi = sem("s_hi")
        s_lo = sem("s_lo")
        s_score = sem("s_score")
        s_score_t = sem("s_score_t")
        s_score_n = sem("s_score_n")
        s_topk = sem("s_topk")
        s_exp = sem("s_exp")
        s_recip = sem("s_recip")
        s_settled = sem("s_settled")
        s_gate = sem("s_gate")
        s_gate_t = sem("s_gate_t")
        s_gate_hi = sem("s_gate_hi")
        s_gate_lo = sem("s_gate_lo")
        s_spread = sem("s_spread")
        s_gate_x = sem("s_gate_x")
        s_h = sem("s_h")
        s_out = sem("s_out")
        s_stored = sem("s_stored")

        def raw_landed(eng, g, n):
            eng.wait_ge(s_raw[n % SLOTS], g * (16 * PIECES // SLOTS) + 16 * (n // SLOTS + 1))

        def u_conv(u, b):
            return u[:, :, b * C:(b + 1) * C].rearrange("p j (g o) -> p g j o", g=CG)

        def ring_conv(item):
            return ring[:, item % SLOTS, :].rearrange("p (g j o) -> p g j o", g=CG, j=PH)

        def load_taps(eng, p):
            j = PH - 1 - p
            eng.dma_start(toep[p * CI:(p + 1) * CI].rearrange("i g h n -> i g (h n)"),
                          taps[:, :, j:j + 2 * PH, :].rearrange("g i j o -> i g (j o)")).then_inc(s_taps, 16)

        def settled(eng):
            eng.sem_inc(s_settled, 1)

        CONV0, MIX0, H0 = 0, 8, 16
        block = ctx.enter_context(nc.Block())

        @block.sync
        def _(sp):
            def load_piece(n):
                sp.dma_start(raw[:, n % SLOTS, :], pieces[n % PIECES]).then_inc(s_raw[n % SLOTS], 16)

            def load_conv_in(g, t):
                sp.dma_start(conv_in[:, 2 * t:2 * t + 2].rearrange("p b g q -> p (b g q)"),
                             conv_x[bass.ds(g, 1), t].rearrange("a p n -> (a p) n")).then_inc(s_convin[t], 16)

            def load_x(g, t):
                sp.dma_start(x1[:, t, :], x[bass.ds(g, 1), t].rearrange("a p n -> (a p) n")).then_inc(s_x, 16)

            for p in range(1, PH, 2):
                load_taps(sp, p)
            sp.dma_start(consts1[:, :], first_consts).then_inc(s_first, 16)
            load_conv_in(0, 0)
            sp.dma_start(hidden_stage, hidden_w).then_inc(s_first, 16)
            load_conv_in(0, 1)
            load_piece(0)
            sp.dma_start(consts2[:, :], later_consts).then_inc(s_later, 16)
            load_conv_in(0, 2)
            load_conv_in(0, 3)
            load_piece(1)
            load_piece(2)
            def group(g, first, last):
                for n in range(PIECES):
                    sp.wait_ge(s_piece_lo, g * PIECES + n + 1)
                    load_piece(n + SLOTS)
                    if n == 0 and first:
                        sp.wait_ge(s_const_hi, 5)
                        sp.wait_ge(s_const_lo, 3)
                        load_x(0, 0)
                        load_x(0, 1)
                        sp.wait_ge(s_p_mixb_bc, 4)
                        load_x(0, 2)
                        load_x(0, 3)
                    if n == 1 and not last:
                        sp.wait_ge(s_conv, g * GB + GB)
                        for t in range(NT):
                            load_conv_in(g + 1, t)
                    if n == 21:
                        store_half(g, 0)
                store_half(g, 1)
                if not last:
                    sp.wait_ge(s_stored, g * (16 * 2 * NT) + 16 * 2 * NT)
                    for t in range(NT):
                        load_x(g + 1, t)

            def store_half(g, h):
                for t in range(NT):
                    sp.wait_ge(s_out, g * 8 + 8 + h * NT + t + 1)
                    sp.dma_start(out[bass.ds(g, 1), t, :, h * HALF:(h + 1) * HALF].rearrange("a p n -> (a p) n"),
                                 x1[:, t, h * HALF:(h + 1) * HALF]).then_inc(s_stored, 16)

            group(0, True, False)
            with sp.Fori(1, GROUPS - 1) as g:
                group(g, False, False)
            group(GROUPS - 1, False, True)
            sp.wait_ge(s_stored, 16 * 2 * NT * GROUPS)
            for n in range(SLOTS):
                sp.wait_ge(s_raw[n], 16 * (GROUPS * PIECES // SLOTS + 1))

        @block.gpsimd
        def _(pool):
            pool.memset(ones[:, :], 1.0).then_inc(s_ones, 1)
            pool.memset(lora_a_r[:, :, :].bitcast(F32), 0.0).then_inc(s_ones, 1)
            pool.memset(lora_s2[:, :].bitcast(F32), 0.0).then_inc(s_ones, 1)
            pool.wait_ge(s_ones, 3)
            pool.memset(lora_s2[96:P, :].bitcast(F32), 1.0).then_inc(s_ones, 1)
            pool.wait_ge(s_ones, 4)
            pool.wait_ge(s_att, 4)
            pool.wait_ge(s_later, 16)
            for k in range(KC):
                weight = att_pair[:, :, k:k + 1].to_broadcast([P, NB // 2, C])
                matrix = mixw[:, k:k + 1, :].to_broadcast([P, NB // 2, C])
                if k == 0:
                    pool.tensor_tensor(agg[:, :, :], weight, matrix, ALU.mult).then_inc(s_agg, 1)
                else:
                    pool.tensor_tensor(agg_part, weight, matrix, ALU.mult).then_inc(s_agg, 1)
                    pool.wait_ge(s_agg, 2 * k)
                    pool.tensor_tensor(agg[:, :, :], agg[:, :, :], agg_part, ALU.add).then_inc(s_agg, 1)
                    pool.wait_ge(s_agg, 2 * k + 1)
            pool.wait_ge(s_const_lo, 3)
            pool.memset(blockdiag[:, :, :], 0.0).then_inc(s_ones, 1)
            pool.wait_ge(s_ones, 5)
            with pool.Fori(0, GROUPS) as g:
                pool.wait_ge(s_conv, g * GB + 1)
                for b in range(2):
                    rows = slice(b * C, (b + 1) * C)
                    pool.tensor_copy(blockdiag[rows, :, rows],
                                     agg[rows, bass.ds(g * NT, NT), :]).then_inc(s_bd, 1)

        @block.scalar
        def _(act):
            for p in range(0, PH, 2):
                load_taps(act, p)
            act.dma_start(lora_a_raw, lora_a).then_inc(s_expand, 16)
            act.dma_start(starts_i[:, :], starts.to_broadcast([P, 4])).then_inc(s_starts, 16)
            act.dma_start(lora_b_stage, lora_b).then_inc(s_expand, 16)
            act.dma_start(wr_raw, wr).then_inc(s_expand, 16)
            act.dma_start(expand_stage, expand).then_inc(s_expand, 16)

            def hidden(n):
                act.wait_ge(s_p_hid, n + 1)
                if n == 0:
                    act.wait_ge(s_first, 32)
                act.activation(hid[:, n, :], banks[0][:, 0:NB], ACT.Gelu, bias=(b0s, b1s)[n]).then_inc(s_hid, 1)

            def spread_quarter(n, to, bank, landed, done):
                act.wait_ge(landed, n + 1)
                act.activation(to[:, n * GB:(n + 1) * GB, :].rearrange("p b c -> p (b c)"), banks[bank][:, :],
                               ACT.Copy).then_inc(done, 1)

            def logits_exp():
                act.wait_ge(s_att, 1)
                act.activation(att[:, 0, :], banks[2][0:NB, 0:KC], ACT.Exp, bias=attstat[:, 0:1],
                               accum_out=attstat[:, 1:2]).then_inc(s_att_exp, 1)

            def const_hi(n):
                act.wait_ge(s_expand, 64)
                act.wait_ge(s_ones, 4)
                to, of = ((lora_a_r[:, :, 0:LORA], lora_a_raw), (lora_m1[:, :], lora_b_stage),
                          (lora_m2[0:LORA_LO, :], x1[0:LORA_LO, 1, :]), (wr_r[:, :, 0:KR_E], wr_raw),
                          (expand_r[:, :], expand_stage))[n]
                act.activation(to, of, ACT.Copy).then_inc(s_const_hi, 1)

            def first_after_conv(b):
                if b == 0:
                    hidden(1)
                    spread_quarter(2, cond_bc, 3, s_p_ctx_bc, s_ctx_bc)
                    spread_quarter(3, cond_bc, 1, s_p_ctx_bc, s_ctx_bc)
                if b == 2:
                    logits_exp()
                if b in (3, 4, 5):
                    split_piece(0, b - 3)
                if b == 6:
                    const_hi(0)

            def split_piece(g, n):
                raw_landed(act, g, n)
                act.activation(piece_hi[:, n % SLOTS, :], raw[:, n % SLOTS, :], ACT.Copy).then_inc(s_piece_hi, 1)

            def next_piece(g, n):
                if 8 <= n < 16:
                    act.wait_ge(s_h, g * NCH + n - 7)
                elif n in (19, 23):
                    act.wait_ge(s_fin, g * 8 + n - 15)
                else:
                    act.wait_ge(s_piece_used, g * 14 + (n if n < 8 else n - 8 - (n > 19)) + 1)
                split_piece(g, n + SLOTS)

            def split_hi(g, item, to, of):
                act.wait_ge(s_ring, g * RING + item + 1)
                act.activation(to, of, ACT.Copy).then_inc(s_hi, 1)

            def group(g, first):
                if first:
                    hidden(0)
                    spread_quarter(0, cond_bc, 1, s_p_ctx_bc, s_ctx_bc)
                    spread_quarter(1, cond_bc, 2, s_p_ctx_bc, s_ctx_bc)
                for b in range(GB):
                    split_hi(g, CONV0 + b, u_conv(u_hi, b), ring_conv(CONV0 + b))
                    if first:
                        first_after_conv(b)
                next_piece(g, 0)
                act.wait_ge(s_lora_masked, g + 1)
                act.activation(lora_s1[0:LORA_M, :], lora_h[0:LORA_M, :], ACT.Identity,
                               bias=ecol[0:LORA_M, 0:1]).then_inc(s_lora_s, 1)
                act.activation(lora_s2[LORA_LO:LORA_M, :], lora_h[0:LORA, :], ACT.Copy).then_inc(s_lora_s, 1)
                if first:
                    for n in range(1, 5):
                        const_hi(n)
                    for n in range(4):
                        spread_quarter(n, mixb_bc, (5, 6, 7, 4)[n], s_p_mixb_bc, s_mixb_bc)
                for n in range(1, 8):
                    next_piece(g, n)
                for c in range(NCH):
                    split_hi(g, MIX0 + c, v_hi[:, c, :], ring[:, (MIX0 + c) % SLOTS, :])
                act.wait_ge(s_score, g + 1)
                act.activation(score_t[:, :], banks[4][:, :], ACT.Copy).then_inc(s_score_t, 1)
                next_piece(g, 8)
                act.wait_ge(s_topk, 7 * g + 3)
                for t in range(NT):
                    act.activation(expd[:, t, :], left[:, 1, t, :], ACT.Exp,
                                   bias=stat[:, 0, t:t + 1]).then_inc(s_exp, 1)
                next_piece(g, 9)
                act.wait_ge(s_gate_t, g + 1)
                act.activation(gate_r[0:KR_E, :], banks[6][0:KR_E, :], ACT.Copy).then_inc(s_gate_hi, 1)
                next_piece(g, 10)

                def spread(c):
                    act.wait_ge(s_spread, g * NCH + c + 1)
                    if c >= 2:
                        act.wait_ge(s_ring, g * RING + H0 + c - 1)
                    act.activation(gate_x[:, c % 2, :], banks[(7, 5)[c % 2]][:, :], ACT.Copy).then_inc(s_gate_x, 1)

                for c in range(0, NCH, 2):
                    spread(c)
                    spread(c + 1)
                    for k in (c, c + 1):
                        split_hi(g, H0 + k, u_hi[:, k, :], ring[:, (H0 + k) % SLOTS, :])
                        if k != c or c == NCH - 2:
                            next_piece(g, 11 + c // 2 + (k == NCH - 1))
                for n in range(16, PIECES):
                    next_piece(g, n)

            group(0, True)
            with act.Fori(1, GROUPS) as g:
                group(g, False)

        @block.vector
        def _(dve):
            dve.wait_ge(s_ones, 4)
            dve.sem_inc(s_out, 8)

            def diagonals(of, step, sem_of):
                dve.wait_ge(sem_of, step)
                dve.tensor_tensor(diag, ident[0:C, None, 0:C].to_broadcast([C, NB, C]),
                                  of[:, :, None].to_broadcast([C, NB, C]), ALU.mult).then_inc(sem_of, 1)

            def context():
                dve.wait_ge(s_first, 32)
                dve.wait_ge(s_p_ctx, 1)
                dve.tensor_scalar(ctxs[0:C, 0, :], banks[3][0:C, 0:NB], fs[0:C], None, ALU.add).then_inc(s_ctx, 1)
                diagonals(ctxs[0:C, 0, :], 1, s_ctx)

            def softmax_max():
                dve.wait_ge(s_p_logit, 1)
                dve.tensor_reduce(attstat[:, 0:1], banks[2][0:NB, 0:KC], AX_X, ALU.max, negate=True).then_inc(s_att, 1)

            def softmax():
                dve.wait_ge(s_att_exp, 1)
                dve.reciprocal(attstat[:, 2:3], attstat[:, 1:2]).then_inc(s_att, 1)
                dve.wait_ge(s_att, 2)
                dve.tensor_scalar(att[:, 1, :], att[:, 0, :], attstat[:, 2:3], None, ALU.mult).then_inc(s_att, 1)
                dve.wait_ge(s_att, 3)
                dve.tensor_tensor(att_diag[0:NB], ident[0:NB, 0:NB, None].to_broadcast([NB, NB, KC]),
                                  att[:, 1, None, :].to_broadcast([NB, NB, KC]), ALU.mult).then_inc(s_mixb, 1)

            def mix_weights():
                dve.wait_ge(s_p_att, 1)
                dve.tensor_copy(att_t[0:KC, :], banks[0][0:KC, 0:NB]).then_inc(s_mixb, 1)
                dve.wait_ge(s_p_att, 2)
                both = banks[1][:, 0:NB * KC].rearrange("p (t b k) -> p t b k", b=2, k=KC)
                dve.tensor_copy(att_pair[0:C], both[0:C, :, 0, :])
                dve.tensor_copy(att_pair[C:P], both[C:P, :, 1, :]).then_inc(s_att, 1)

            def mix_bias():
                dve.wait_ge(s_p_att, 3)
                dve.tensor_copy(ctxs[0:C, 1, :], banks[3][0:C, 0:NB]).then_inc(s_mixb, 1)
                dve.wait_ge(s_p_ctx_bc, 4)
                diagonals(ctxs[0:C, 1, :], 3, s_mixb)

            def adapters():
                step = 0

                def then(ins, wait=True):
                    nonlocal step
                    ins.then_inc(s_adapter, 1)
                    step += 1
                    if wait:
                        dve.wait_ge(s_adapter, step)

                dve.wait_ge(s_later, 16)
                dve.wait_ge(s_starts, 16)
                then(dve.tensor_copy(starts_f[:, :], starts_i[:, :]))
                for n in range(4):
                    then(dve.tensor_scalar(reached[:, n, :], brow, starts_f[:, n:n + 1], None, ALU.is_ge), n == 3)
                low, high = count[:, 0, :], count[:, 1, :]
                then(dve.tensor_scalar(low, reached[:, 0, :], -1.0, 2.0, ALU.mult, ALU.add))
                then(dve.tensor_tensor(low, low, reached[:, 1, :], ALU.mult))
                then(dve.tensor_tensor(low, low, reached[:, 0, :], ALU.add))
                then(dve.scalar_tensor_tensor(out=high, in0=reached[:, 3, :], scalar=3.0, in1=low,
                                              op0=ALU.add, op1=ALU.subtract))
                then(dve.tensor_tensor(high, high, reached[:, 2, :], ALU.mult))
                then(dve.tensor_tensor(high, high, low, ALU.add))
                then(dve.tensor_scalar(lora_mask[:, :], high, 2.0, acol, ALU.subtract, ALU.is_equal))

            def const_lo(n):
                dve.wait_ge(s_const_hi, (1, 2, 4)[n])
                to, of, hi = ((lora_a_r[:, :, LORA_LO:LORA_M], lora_a_raw, lora_a_r[:, :, 0:LORA]),
                              (lora_m2[LORA_LO:P, :], x1[LORA_LO:P, 1, :], lora_m1[LORA_LO:P, :]),
                              (wr_r[:, :, KR_E:P], wr_raw, wr_r[:, :, 0:KR_E]))[n]
                dve.tensor_tensor(to, of, hi.bitcast(F32), ALU.subtract).then_inc(s_const_lo, 1)

            def first_after_conv(b):
                if b == 1:
                    softmax_max()
                if b == 2:
                    softmax()
                if b == 3:
                    adapters()
                if b == 4:
                    mix_weights()
                if b in (4, 5, 6):
                    split_piece(0, b - 4)
                if b == 6:
                    mix_bias()
                if b == 7:
                    const_lo(0)

            def split_piece(g, n):
                dve.wait_ge(s_piece_hi, g * PIECES + n + 1)
                dve.tensor_tensor(piece_lo[:, n % SLOTS, :], raw[:, n % SLOTS, :],
                                  piece_hi[:, n % SLOTS, :].bitcast(F32), ALU.subtract).then_inc(s_piece_lo, 1)

            def ring_free(g, item):
                dve.wait_ge(s_lo, g * RING + item + 1)

            def split_lo(g, item, to, of, hi):
                dve.wait_ge(s_hi, g * RING + item + 1)
                dve.tensor_tensor(to, of, hi, ALU.subtract).then_inc(s_lo, 1)

            dve.sem_inc(s_lo, SLOTS)

            def group(g, first):
                def conv_lo(b):
                    split_lo(g, CONV0 + b, u_conv(u_lo, b), ring_conv(CONV0 + b), u_conv(u_hi, b).bitcast(F32))

                for b in range(GB):
                    if first and b == 0:
                        context()
                    dve.wait_ge(s_conv, g * GB + b + 1)
                    if b == 0:
                        dve.wait_ge(s_ctx_bc, 1)
                    ring_free(g, CONV0 + b)
                    bias = cond_bc[:, bass.ds(g * GB + b, 1), :].rearrange("p a (g o) -> p (a g) o", g=CG)
                    dve.tensor_tensor(ring_conv(CONV0 + b),
                                      banks[4 + b % 4][:, :].rearrange("p (g j o) -> p g j o", g=CG, j=PH),
                                      bias[:, :, None, :].to_broadcast([P, CG, PH, CI]), ALU.add).then_inc(s_ring, 1)
                    if b:
                        conv_lo(b - 1)
                    if first:
                        first_after_conv(b)
                conv_lo(GB - 1)
                split_piece(g, SLOTS)
                dve.wait_ge(s_lora_h, g + 1)
                mask = lora_mask[0:LORA_M, bass.ds(g * GB, GB)]
                dve.tensor_tensor(lora_h[0:LORA_M, :].rearrange("p (b c) -> p b c", b=GB),
                                  banks[4][0:LORA_M, :].rearrange("p (b c) -> p b c", b=GB),
                                  mask[:, :, None].to_broadcast([LORA_M, GB, C]), ALU.mult).then_inc(s_lora_masked, 1)
                dve.wait_ge(s_lora_s, 2 * g + 1)
                dve.wait_ge(s_lora_masked, g + 1)
                dve.tensor_tensor(lora_s2[0:LORA, :], lora_h[0:LORA, :], lora_s1[0:LORA, :].bitcast(F32),
                                  ALU.subtract).then_inc(s_lora_lo, 1)
                if first:
                    const_lo(1)
                    const_lo(2)
                split_piece(g, 4)
                split_piece(g, 5)
                dve.wait_ge(s_x, g * (16 * NT) + 16 * NT)
                for h in range(2):
                    for t in range(NT):
                        dve.wait_ge(s_ffn, g * 8 + h * NT + t + 1)
                        half = x1[:, t, h * HALF:(h + 1) * HALF]
                        dve.tensor_tensor(half, half, banks[4 * h + t][:, :], ALU.add).then_inc(s_x1, 1)
                    for n in ((6, 7, 8, 9), ())[h]:
                        split_piece(g, n)

                if first:
                    dve.wait_ge(s_mixb_bc, 4)

                def mix_lo(c):
                    split_lo(g, MIX0 + c, v_lo[:, c, :], ring[:, (MIX0 + c) % SLOTS, :], v_hi[:, c, :].bitcast(F32))

                for c in range(NCH):
                    dve.wait_ge(s_mix, g * NCH + c + 1)
                    ring_free(g, MIX0 + c)
                    bias = mixb_bc[:, bass.ds(g * GB, GB), :].rearrange("p b c -> p (b c)")
                    dve.tensor_tensor(ring[:, (MIX0 + c) % SLOTS, :], banks[1 + c % 3][:, :], bias,
                                      ALU.add).then_inc(s_ring, 1)
                    if c >= 2:
                        mix_lo(c - 2)
                mix_lo(NCH - 2)
                mix_lo(NCH - 1)
                split_piece(g, 10)
                dve.wait_ge(s_score_n, g + 1)
                scores = left[:, 1, :, :]
                dve.tensor_reduce(scores.rearrange("p t e -> p (t e)"),
                                  banks[5][:, :].rearrange("p (t a e) -> p t e a", t=NT, a=2), AX_X,
                                  ALU.add).then_inc(s_topk, 1)
                dve.wait_ge(s_topk, 7 * g + 1)
                settled(dve)
                for t in range(NT):
                    last = dve.max(top[:, t, 0:8], scores[:, t, :])
                last.then_inc(s_topk, 1)
                dve.wait_ge(s_topk, 7 * g + 2)
                dve.tensor_scalar(stat[:, 0, :], top[:, :, 0:1].rearrange("p t a -> p (t a)"), -1.0, None,
                                  ALU.mult).then_inc(s_topk, 1)
                settled(dve)
                for t in range(NT):
                    last = dve.match_replace(left[:, 0, t, :], top[:, t, 0:8], scores[:, t, :], NEG)
                last.then_inc(s_topk, 1)
                dve.wait_ge(s_topk, 7 * g + 4)
                settled(dve)
                for t in range(NT):
                    last = dve.max(top[:, t, 8:16], left[:, 0, t, :])
                last.then_inc(s_topk, 1)
                dve.wait_ge(s_exp, g * NT + NT)
                settled(dve)
                dve.wait_ge(s_topk, 7 * g + 5)
                settled(dve)
                for t in range(NT):
                    last = dve.match_replace(left[:, 1, t, :], top[:, t, 8:16], left[:, 0, t, :], NEG)
                last.then_inc(s_topk, 1)
                dve.wait_ge(s_topk, 7 * g + 6)
                for t in range(NT):
                    last = dve.scalar_tensor_tensor(out=expd[:, t, :], in0=left[:, 1, t, :], scalar=NEG,
                                                    in1=expd[:, t, :], op0=ALU.is_equal, op1=ALU.mult,
                                                    accum_out=stat[:, 1, t:t + 1])
                last.then_inc(s_topk, 1)
                dve.wait_ge(s_topk, 7 * g + 7)
                dve.reciprocal(stat[:, 2, :], stat[:, 1, :]).then_inc(s_recip, 1)
                dve.wait_ge(s_recip, g + 1)
                for t in range(NT):
                    dve.tensor_scalar(gate[:, t, :], expd[:, t, :], stat[:, 2, t:t + 1], 2.0, ALU.mult,
                                      ALU.mult).then_inc(s_gate, 1)
                split_piece(g, 11)
                split_piece(g, 12)
                dve.wait_ge(s_gate_t, g + 1)
                dve.wait_ge(s_gate_hi, g + 1)
                dve.tensor_tensor(gate_r[KR_E:P, :], banks[6][0:KR_E, :], gate_r[0:KR_E, :].bitcast(F32),
                                  ALU.subtract).then_inc(s_gate_lo, 1)
                split_piece(g, 13)

                def gated(c):
                    dve.wait_ge(s_h, g * NCH + c + 1)
                    dve.wait_ge(s_gate_x, g * NCH + c + 1)
                    ring_free(g, H0 + c)
                    dve.tensor_tensor(ring[:, (H0 + c) % SLOTS, :], banks[c % 4][:, :], gate_x[:, c % 2, :],
                                      ALU.mult).then_inc(s_ring, 1)

                for c in range(0, NCH, 2):
                    for k in (c, c + 1):
                        if c < NCH - 2:
                            gated(k)
                    for k in (c, c + 1):
                        if c == NCH - 2:
                            gated(k)
                        split_lo(g, H0 + k, u_lo[:, k, :], ring[:, (H0 + k) % SLOTS, :], u_hi[:, k, :].bitcast(F32))
                        if k != c or c == NCH - 2:
                            split_piece(g, 14 + c // 2 + (k == NCH - 1))
                for h in range(2):
                    for n in ((19, 20, 21), (22, 23, 24, 25))[h]:
                        split_piece(g, n)
                    for t in range(NT):
                        dve.wait_ge(s_fin, g * 8 + h * NT + t + 1)
                        half = x1[:, t, h * HALF:(h + 1) * HALF]
                        dve.tensor_tensor(half, half, banks[4 - 4 * h + t][:, :], ALU.add).then_inc(s_out, 1)
                split_piece(g, 26)

            group(0, True)
            dve.wait_ge(s_ctx_bc, 4)
            with dve.Fori(1, GROUPS) as g:
                group(g, False)

        @block.tensor
        def _(pe):
            def context():
                pe.wait_ge(s_first, 16 * 2)
                pe.matmul(banks[3][0:C, 0:NB], cw_t, cond_t, start=True, stop=True).then_inc(s_p_ctx, 1)

            def hidden(n):
                if n:
                    pe.wait_ge(s_hid, 1)
                pe.matmul(banks[0][:, 0:NB], (w0s, w1s)[n], (cond_t, hid[:, 0, :])[n], start=True,
                          stop=True).then_inc(s_p_hid, 1)

            def logits():
                pe.wait_ge(s_hid, 2)
                pe.wait_ge(s_ctx_bc, 2)
                pe.matmul(banks[2][0:NB, 0:KC], hid[:, 1, :], w2s, start=True, stop=False)
                pe.matmul(banks[2][0:NB, 0:KC], ones[0:1, 0:NB], b2s[0:1, :], start=False,
                          stop=True).then_inc(s_p_logit, 1)

            def spread_diag(n, bank, sem_of):
                pe.matmul(banks[bank][:, :], ones[0:C, :], diag[:, n * GB:(n + 1) * GB, :].rearrange("p b c -> p (b c)"),
                          start=True, stop=True).then_inc(sem_of, 1)

            def first_after_conv(b):
                if b == 0:
                    pe.wait_ge(s_ones, 1)
                    pe.wait_ge(s_ctx, 2)
                    spread_diag(0, 1, s_p_ctx_bc)
                    spread_diag(1, 2, s_p_ctx_bc)
                if b == 1:
                    hidden(1)
                if b == 2:
                    spread_diag(2, 3, s_p_ctx_bc)
                    pe.wait_ge(s_ctx_bc, 1)
                    spread_diag(3, 1, s_p_ctx_bc)
                if b == 3:
                    logits()
                if b == 5:
                    pe.wait_ge(s_mixb, 1)
                    pe.transpose(banks[0][0:KC, 0:NB], att[:, 1, :], ident[0:NB, 0:NB]).then_inc(s_p_att, 1)
                    pe.wait_ge(s_ctx_bc, 4)
                    pe.matmul(banks[1][:, 0:NB * KC], ones[0:NB, :], att_diag[0:NB].rearrange("p b k -> p (b k)"),
                              start=True, stop=True).then_inc(s_p_att, 1)
                if b == 6:
                    pe.wait_ge(s_mixb, 2)
                    pe.wait_ge(s_later, 16)
                    pe.matmul(banks[3][0:C, 0:NB], mixb[0:KC, :], att_t[0:KC, :], start=True, stop=True).then_inc(s_p_att, 1)

            def product(to, left_hi, left_lo, right_hi, right_lo, first, last):
                pe.matmul(to, left_hi, right_hi, start=first, stop=False)
                pe.matmul(to, left_hi, right_lo, start=False, stop=False)
                return pe.matmul(to, left_lo, right_hi, start=False, stop=last)

            def piece_ready(g, n):
                pe.wait_ge(s_piece_lo, g * PIECES + n + 1)

            def split_done(g, item):
                pe.wait_ge(s_lo, g * RING + item + 1 + SLOTS)

            def columns_piece(n, c):
                return (piece_hi[:, n % SLOTS, c * HALF:(c + 1) * HALF], piece_lo[:, n % SLOTS, c * HALF:(c + 1) * HALF])

            def group(g, first):
                if first:
                    context()
                    hidden(0)
                    pe.wait_ge(s_taps, 16 * PH)
                for b in range(GB):
                    if b % 2 == 0:
                        pe.wait_ge(s_convin[b // 2], g * 16 + 16)
                    if b < 4:
                        pe.wait_ge(s_out, g * 8 + b + 1)
                    else:
                        pe.wait_ge(s_ring, g * RING + CONV0 + b - 3)
                    for cg in range(CG):
                        for h in range(2):
                            mm = pe.matmul(banks[4 + b % 4][:, cg * P:(cg + 1) * P], conv_in[:, b, cg, h:h + Q],
                                           toep[:, cg, 1 - h, :], start=(h == 0), stop=(h == 1))
                    mm.then_inc(s_conv, 1)
                    if first:
                        first_after_conv(b)

                def ffn_piece(n):
                    h, j = n // 4, n % 4
                    piece_ready(g, n)
                    for t in range(NT):
                        if n == 0:
                            pe.wait_ge(s_out, g * 8 + 4 + t + 1)
                            split_done(g, CONV0 + 2 * t + 1)
                        for c in range(2):
                            k = 2 * j + c
                            mm = product(banks[4 * h + t][:, :], u_hi[:, k, t * P:(t + 1) * P],
                                         u_lo[:, k, t * P:(t + 1) * P], *columns_piece(n, c), k == 0, False)
                        if t == NT - 1:
                            mm.then_inc(s_piece_used, 1)
                        if j == 3:
                            lora_second(h, t)

                def lora_second(h, t):
                    if t == 0:
                        pe.wait_ge(s_lora_s, 2 * g + 2)
                        pe.wait_ge(s_lora_lo, g + 1)
                        if first and h == 0:
                            pe.wait_ge(s_const_hi, 3)
                            pe.wait_ge(s_const_lo, 2)
                    pe.matmul(banks[4 * h + t][:, :], lora_s1[0:LORA_M, t * P:(t + 1) * P],
                              lora_m1[0:LORA_M, h * HALF:(h + 1) * HALF], start=False, stop=False)
                    pe.matmul(banks[4 * h + t][:, :], lora_s2[0:LORA_M + 1, t * P:(t + 1) * P],
                              lora_m2[0:LORA_M + 1, h * HALF:(h + 1) * HALF], start=False,
                              stop=True).then_inc(s_ffn, 1)

                ffn_piece(0)
                if first:
                    pe.wait_ge(s_const_lo, 1)
                for k in range(NCH):
                    for part in (u_hi, u_lo):
                        mm = pe.matmul(banks[4][0:LORA_M, :], lora_a_r[:, k, :], part[:, k, :],
                                       start=(k == 0 and part is u_hi), stop=(k == NCH - 1 and part is u_lo))
                mm.then_inc(s_lora_h, 1)
                if first:
                    pe.wait_ge(s_mixb, 4)
                    for n in range(3):
                        pe.wait_ge(s_ring, CONV0 + 6 + n)
                        spread_diag(n, 5 + n, s_p_mixb_bc)
                    pe.wait_ge(s_lora_masked, 1)
                    spread_diag(3, 4, s_p_mixb_bc)
                for n in (1, 2, 3):
                    ffn_piece(n)
                if first:
                    pe.wait_ge(s_mixb_bc, 4)
                pe.wait_ge(s_lora_masked, g + 1)
                for n in (4, 5, 6, 7):
                    ffn_piece(n)

                def mix(c):
                    if c == 0:
                        pe.wait_ge(s_bd, 2 * g + 2)
                        pe.wait_ge(s_x1, g * 8 + 4)
                    if c == 4:
                        pe.wait_ge(s_x1, g * 8 + 8)
                    if c >= 3:
                        pe.wait_ge(s_ring, g * RING + MIX0 + c - 2)
                    for t in range(NT):
                        mm = pe.matmul(banks[1 + c % 3][:, t * P:(t + 1) * P], x1[:, t, c * P:(c + 1) * P],
                                       blockdiag[:, t, :], start=True, stop=True)
                    mm.then_inc(s_mix, 1)

                def score(c):
                    split_done(g, MIX0 + c)
                    if first and c == 0:
                        pe.wait_ge(s_const_lo, 3)
                    if c == 0:
                        pe.wait_ge(s_x1, g * 8 + 5)
                    pe.matmul(banks[4][:, :], wr_r[:, c, :], v_hi[:, c, :], start=(c == 0), stop=False)
                    mm = pe.matmul(banks[4][:, :], wr_r[:, c, :], v_lo[:, c, :], start=False, stop=(c == NCH - 1))
                    if c == NCH - 1:
                        mm.then_inc(s_score, 1)

                def h_part(c, ks):
                    n = 8 + c
                    if ks[0] == 0:
                        piece_ready(g, n)
                        if c >= 4:
                            pe.wait_ge(s_ring, g * RING + H0 + c - 3)
                    for k in ks:
                        if c == 0:
                            split_done(g, MIX0 + k)
                        cols = slice(k * P, (k + 1) * P)
                        mm = product(banks[c % 4][:, :], piece_hi[:, n % SLOTS, cols], piece_lo[:, n % SLOTS, cols],
                                     v_hi[:, k, :], v_lo[:, k, :], k == 0, k == NCH - 1)
                    if ks[-1] == NCH - 1:
                        mm.then_inc(s_h, 1)

                def spread(c):
                    if c == 0:
                        pe.wait_ge(s_gate_hi, g + 1)
                        pe.wait_ge(s_gate_lo, g + 1)
                    if c >= 2:
                        pe.wait_ge(s_gate_x, g * NCH + c - 1)
                    pe.matmul(banks[(7, 5)[c % 2]][:, :], expand_r[:, c * P:(c + 1) * P], gate_r[:, :],
                              start=True, stop=True).then_inc(s_spread, 1)

                for c in range(NCH + LAG):
                    if c < NCH:
                        mix(c)
                    if c >= LAG:
                        score(c - LAG)
                        h_part(0, (c - LAG,))
                pe.wait_ge(s_score_t, g + 1)
                for t in range(NT):
                    mm = pe.transpose(banks[5][:, t * P:(t + 1) * P], score_t[:, t * P:(t + 1) * P], ident)
                mm.then_inc(s_score_n, 1)
                front, back = (0, 1, 2, 3), (4, 5, 6, 7)
                h_part(1, front + back)
                h_part(2, front + back)
                for t in range(NT):
                    pe.wait_ge(s_gate, g * NT + t + 1)
                    settled(pe)
                    mm = pe.transpose(banks[6][0:KR_E, t * P:(t + 1) * P], gate[:, t, :], ident)
                mm.then_inc(s_gate_t, 1)
                for c in range(3, NCH):
                    h_part(c, front)
                    if c < 7:
                        spread(2 * (c - 3))
                        spread(2 * (c - 3) + 1)
                    h_part(c, back)

                for n in range(16, PIECES):
                    h, j = (n - 16) // 4, n % 4
                    piece_ready(g, n)
                    if n == 16:
                        pe.wait_ge(s_gate_x, g * NCH + NCH)
                    if h == 0:
                        split_done(g, H0 + 2 * j + 1)
                    for t in range(NT):
                        for c in range(2):
                            k = 2 * j + c
                            mm = product(banks[4 - 4 * h + t][:, :], u_hi[:, k, t * P:(t + 1) * P],
                                         u_lo[:, k, t * P:(t + 1) * P], *columns_piece(n, c), k == 0, k == NCH - 1)
                        if j < 3 and t == NT - 1:
                            mm.then_inc(s_piece_used, 1)
                        if j == 3:
                            mm.then_inc(s_fin, 1)

            group(0, True)
            with pe.Fori(1, GROUPS) as g:
                group(g, False)


def kernel(x, cond_128, fside_S_0, L0_cond_weight, L0_cond_c_weight, L0_ffn_weight, L0_ffn_bias,
           L0_ffn_lora_A, L0_ffn_lora_B, L0_ffn_lora_start_indices, L1_cond_W0, L1_cond_b0, L1_cond_W1,
           L1_cond_b1, L1_cond_W2, L1_cond_b2, L1_cond_weight, L1_cond_bias_k, L1_ffn_A, L1_ffn_B, L1_ffn_Wr):
    import numpy as np
    import concourse.bacc as bacc
    from concourse.bass_utils import run_bass_kernel_spmd

    x = np.asarray(x)
    padded = np.pad(x, ((0, 0), (0, 0), (TAPS // 2, TAPS // 2)))
    conv_x = padded.reshape(GROUPS, NT, 2, CG, CI, Q + 1, PH).transpose(0, 1, 6, 4, 2, 3, 5)
    taps = np.asarray(L0_cond_weight).reshape(CG, CI, CI, TAPS).transpose(0, 2, 3, 1)[:, :, ::-1, :]
    taps = np.pad(taps, ((0, 0), (0, 0), (PH - 1, PH - 1), (0, 0)))
    w = np.asarray(L0_ffn_weight).reshape(2, HALF, Q, 4, 2).transpose(0, 3, 2, 4, 1).reshape(8, P, L)
    a = np.asarray(L1_ffn_A).reshape(NCH, P, NCH, P).transpose(0, 3, 2, 1).reshape(8, P, L)
    b = (np.asarray(L1_ffn_B).transpose(0, 2, 1).reshape(4, 2, P, 2, HALF)
         .transpose(3, 0, 2, 1, 4).reshape(8, P, L))
    eye = np.eye(P, dtype=np.float32)
    rows = np.arange(P)
    adapter = (rows % LORA_LO) // RANK

    def side_by_side(names, parts):
        for (name, width), part in zip(names, parts, strict=True):
            assert part.shape[1] == width, name
        return np.concatenate([np.pad(v, ((0, P - v.shape[0]), (0, 0))) for v in parts], axis=1)

    mix_w = np.asarray(L1_cond_weight).reshape(KC, C, C).transpose(2, 0, 1).reshape(C, KC * C)
    adapters = np.asarray(L0_ffn_lora_B).transpose(0, 2, 1).reshape(LORA, L)
    adapters = np.pad(np.concatenate([adapters, np.asarray(L0_ffn_bias).reshape(1, L)]),
                      ((0, LORA_LO - LORA - 1), (0, 0)))
    arrays = {
        "conv_x": conv_x.reshape(GROUPS, NT, P, 2 * CG * (Q + 1)),
        "x": x.reshape(GROUPS, NT, P, L),
        "taps": taps,
        "pieces": np.concatenate([w, a, b]),
        "first_consts": side_by_side(FIRST, [
            eye, np.asarray(cond_128).T, np.asarray(L0_cond_c_weight).T, np.asarray(fside_S_0).reshape(C, 1),
            np.asarray(L1_cond_b0).reshape(P, 1), np.asarray(L1_cond_b1).reshape(P, 1),
            np.asarray(L1_cond_W2), np.asarray(L1_cond_b2).reshape(1, KC)]),
        "hidden_w": np.concatenate([np.asarray(L1_cond_W0), np.asarray(L1_cond_W1)], axis=1),
        "later_consts": side_by_side(LATER, [
            np.asarray(L1_cond_bias_k), np.tile(np.arange(NB, dtype=np.float32), (P, 1)),
            adapter.astype(np.float32).reshape(P, 1), (rows == LORA).astype(np.float32).reshape(P, 1),
            np.concatenate([mix_w, mix_w])]),
        "lora_a": np.asarray(L0_ffn_lora_A).reshape(LORA, Q, PH).transpose(1, 2, 0),
        "lora_b": np.concatenate([adapters, adapters]),
        "starts": np.asarray(L0_ffn_lora_start_indices).reshape(1, 4),
        "wr": np.asarray(L1_ffn_Wr).reshape(KR_E, NCH, P).transpose(2, 1, 0),
        "expand": np.tile(np.repeat(np.eye(KR_E, dtype=np.float32), RANK, axis=1), (2, 1)),
    }
    nc = bacc.Bacc("TRN2", target_bir_lowering=False, num_devices=1)
    aps = {}
    for name, v in arrays.items():
        arrays[name] = v = np.ascontiguousarray(v)
        aps[name] = nc.dram_tensor(name, v.shape, mybir.dt.from_np(v.dtype), kind="ExternalInput").ap()
    out = nc.dram_tensor("out", (GROUPS, NT, P, L), F32, kind="ExternalOutput").ap()
    adaln_ffn_kernel(nc, **aps, out=out)
    result = run_bass_kernel_spmd(nc, [arrays], core_ids=[0]).results[0]["out"]
    return result.reshape(NB, C, L)
```

```python
from contextlib import ExitStack

import concourse.bass as bass
from concourse import mybir

F32 = mybir.dt.float32
F32R = mybir.dt.float32r
I32 = mybir.dt.int32
ALU = mybir.AluOpType
ACT = mybir.ActivationFunctionType
AX_X = mybir.AxisListType.X

P = 128
NB, C, L = 32, 64, 1024
GROUPS = 4
GB = NB // GROUPS
NT = GB * C // P
TOK = NT * P
CG, CI, TAPS = 4, 16, 9
PH = 8
Q = L // PH
NCH = L // P
HALF = 512
KR_E, RANK, TOPK = 64, 16, 16
LORA = 3 * 16
FIRST = (("ident", 128), ("cond", 32), ("c_weight", 64), ("fside", 1), ("frow", 64), ("b0", 1), ("b1", 1), ("w2", 8), ("b2", 8))
LATER = (("mix_b", 64), ("batch_row", 32), ("adapter", 1), ("one", 1), ("mix_w", 512))
LORA_LO = 64
LORA_M = LORA_LO + LORA
KC = 8
PIECES = 24
SLOTS = 3
RING = 24
LAG = 3
WARM_UP = 12
NEG = -3.0e38


def adaln_ffn_kernel(nc, conv_x, x, taps, pieces, first_consts, hidden_w, later_consts, lora_a, lora_b,
                     starts, wr, expand, spread, out):
    with ExitStack() as ctx:
        def sb(name, shape, dt=F32):
            return ctx.enter_context(nc.sbuf_tensor(name, shape, dt))

        def sem(name):
            return ctx.enter_context(nc.semaphore(name))

        raw = sb("raw", [P, SLOTS, L])
        piece_hi = sb("piece_hi", [P, SLOTS, L], F32R)
        piece_lo = sb("piece_lo", [P, SLOTS, L], F32R)
        x1 = sb("x1", [P, NT, L])
        conv_in = sb("conv_in", [P, GB, CG, Q + 1])
        u_hi = sb("u_hi", [P, NCH, TOK], F32R)
        u_lo = sb("u_lo", [P, NCH, TOK], F32R)
        v_hi = sb("v_hi", [P, NCH, TOK], F32R)
        v_lo = sb("v_lo", [P, NCH, TOK], F32R)
        ring = sb("ring", [P, SLOTS, TOK])
        toep = sb("toep", [P, CG, 2, P])
        ones = sb("ones", [P, P])
        cond_bc = sb("cond_bc", [P, NB, C])
        mixb_bc = sb("mixb_bc", [P, NB, C])
        agg = sb("agg", [P, NB // 2, C])
        blockdiag = sb("blockdiag", [P, NT, P])
        expand_r = sb("expand_r", [P, L], F32R)
        lora_a_r = sb("lora_a_r", [P, PH, LORA_M], F32R)
        lora_m1 = sb("lora_m1", [P, L], F32R)
        lora_m2 = sb("lora_m2", [P, L], F32R)
        wr_r = sb("wr_r", [P, NCH, P], F32R)
        lora_h = sb("lora_h", [P, TOK])
        lora_s1 = sb("lora_s1", [P, TOK], F32R)
        lora_s2 = sb("lora_s2", [P, TOK], F32R)
        lora_mask = sb("lora_mask", [P, NB])
        score_t = sb("score_t", [P, TOK])
        top = sb("top", [P, NT, 16])
        left = sb("left", [P, 2, NT, KR_E])
        expd = sb("expd", [P, NT, KR_E])
        gate = sb("gate", [P, NT, KR_E])
        stat = sb("stat", [P, 3, NT])
        gate_r = sb("gate_r", [P, TOK], F32R)
        gate_x = sb("gate_x", [P, 2, TOK])
        consts1 = sb("consts1", [P, sum(w for _, w in FIRST)])
        consts2 = sb("consts2", [P, sum(w for _, w in LATER)])
        starts_i = sb("starts_i", [P, 4], I32)
        starts_f = sb("starts_f", [P, 4])
        hid = sb("hid", [P, 2, NB])
        ctx_t = sb("ctx_t", [P, GB])
        biases = sb("biases", [NB, 2, C])
        att = sb("att", [NB, 3, KC])
        attstat = sb("attstat", [NB, 3])
        att_t = sb("att_t", [P, NB])
        att_pair = sb("att_pair", [P, NB // 2, KC])

        def columns(tile, names, name):
            at = 0
            for n, w in names:
                if n == name:
                    return tile[:, at:at + w]
                at += w

        ident, cond_t, cw_t, fs, frow, b0s, b1s, w2s, b2s = (columns(consts1, FIRST, n) for n, _ in FIRST)
        mixb, brow, acol, ecol, mixw = (columns(consts2, LATER, n) for n, _ in LATER)
        mixw = mixw.rearrange("p (k c) -> p k c", c=C)
        agg_part = gate_x[:, :, :].rearrange("p a (b c) -> p (a b) c", c=C)
        lora_a_raw = score_t[:, 0:PH * LORA].rearrange("p (k m) -> p k m", m=LORA)
        wr_raw = blockdiag[:, :, :].rearrange("p t n -> p (t n)").rearrange("p (k m) -> p k m", m=KR_E)
        w0s = gate[:, 0:2, :].rearrange("p t e -> p (t e)")
        w1s = gate[:, 2:4, :].rearrange("p t e -> p (t e)")
        hidden_stage = gate[:, :, :].rearrange("p t e -> p (t e)")
        att_diag = expd[:, :, :].rearrange("p t e -> p (t e)").rearrange("p (b k) -> p b k", k=KC)
        reached = left[:, 0, 0:2, :].rearrange("p t e -> p (t e)").rearrange("p (n b) -> p n b", b=NB)
        count = left[:, 0, 2, :].rearrange("p (n b) -> p n b", b=NB)
        expand_stage, lora_b_stage = x1[:, 0, :], x1[:, 1, :]
        diag = x1[0:C, 2, 0:GB * C].rearrange("p (b c) -> p b c", b=GB)

        banks = [ctx.enter_context(nc.psum_tensor(f"bank{i}", [P, HALF], F32)) for i in range(8)]

        s_first = sem("s_first")
        s_taps = sem("s_taps")
        s_later = sem("s_later")
        s_starts = sem("s_starts")
        s_expand = sem("s_expand")
        s_ones = sem("s_ones")
        s_p_ctx = sem("s_p_ctx")
        s_p_hid = sem("s_p_hid")
        s_p_logit = sem("s_p_logit")
        s_p_ctx_bc = sem("s_p_ctx_bc")
        s_p_att = sem("s_p_att")
        s_hid = sem("s_hid")
        s_att_exp = sem("s_att_exp")
        s_ctx_bc = sem("s_ctx_bc")
        s_out_ctx = sem("s_out_ctx")
        s_out_mixb = sem("s_out_mixb")
        s_rest_bc = sem("s_rest_bc")
        s_mixb_bc = sem("s_mixb_bc")
        s_const_hi = sem("s_const_hi")
        s_ctx = sem("s_ctx")
        s_att = sem("s_att")
        s_mixb = sem("s_mixb")
        s_adapter = sem("s_adapter")
        s_const_lo = sem("s_const_lo")
        s_agg = sem("s_agg")
        s_raw = [sem(f"s_raw{i}") for i in range(SLOTS)]
        s_piece_hi = sem("s_piece_hi")
        s_piece_lo = sem("s_piece_lo")
        s_piece_used = sem("s_piece_used")
        s_convin = [sem(f"s_convin{t}") for t in range(NT)]
        s_x = sem("s_x")
        s_conv = sem("s_conv")
        s_lora_h = sem("s_lora_h")
        s_lora_masked = sem("s_lora_masked")
        s_lora_s = sem("s_lora_s")
        s_lora_lo = sem("s_lora_lo")
        s_ffn = sem("s_ffn")
        s_fin = sem("s_fin")
        s_x1 = sem("s_x1")
        s_bd = sem("s_bd")
        s_mix = sem("s_mix")
        s_ring = sem("s_ring")
        s_hi = sem("s_hi")
        s_lo = sem("s_lo")
        s_score = sem("s_score")
        s_score_t = sem("s_score_t")
        s_score_n = sem("s_score_n")
        s_topk = sem("s_topk")
        s_exp = sem("s_exp")
        s_recip = sem("s_recip")
        s_settled = sem("s_settled")
        s_gate = sem("s_gate")
        s_gate_t = sem("s_gate_t")
        s_gate_hi = sem("s_gate_hi")
        s_gate_lo = sem("s_gate_lo")
        s_spread = sem("s_spread")
        s_gate_x = sem("s_gate_x")
        s_h = sem("s_h")
        s_out = sem("s_out")
        s_stored = sem("s_stored")

        def raw_landed(eng, g, n):
            eng.wait_ge(s_raw[n % SLOTS], g * (16 * PIECES // SLOTS) + 16 * (n // SLOTS + 1))

        def u_conv(u, b):
            return u[:, :, b * C:(b + 1) * C].rearrange("p j (g o) -> p g j o", g=CG)

        def ring_conv(item):
            return ring[:, item % SLOTS, :].rearrange("p (g j o) -> p g j o", g=CG, j=PH)

        def load_taps(eng, cg):
            tap, ci = CI, taps.shape[2] * CI
            windows = bass.AP(taps.tensor, taps.offset + cg * CI * ci, [[tap, PH], [ci, CI], [1, 2 * P]])
            eng.dma_start(toep[:, cg].rearrange("r h n -> r (h n)"), windows).then_inc(s_taps, 16)

        def settled(eng):
            eng.sem_inc(s_settled, 1)

        CONV0, MIX0, H0 = 0, 8, 16
        block = ctx.enter_context(nc.Block())

        @block.sync
        def _(sp):
            def load_piece(n):
                sp.dma_start(raw[:, n % SLOTS, :], pieces[n % PIECES]).then_inc(s_raw[n % SLOTS], 16)

            def load_conv_in(g, t):
                sp.dma_start(conv_in[:, 2 * t:2 * t + 2].rearrange("p b g q -> p (b g q)"),
                             conv_x[bass.ds(g, 1), t].rearrange("a p n -> (a p) n")).then_inc(s_convin[t], 16)

            def load_x(g, t):
                sp.dma_start(x1[:, t, :], x[bass.ds(g, 1), t].rearrange("a p n -> (a p) n")).then_inc(s_x, 16)

            load_conv_in(0, 0)
            load_taps(sp, 2)
            load_taps(sp, 3)
            sp.dma_start(hidden_stage, hidden_w).then_inc(s_first, 16)
            load_conv_in(0, 1)
            load_piece(0)
            sp.dma_start(consts2[:, :], later_consts).then_inc(s_later, 16)
            load_conv_in(0, 2)
            load_conv_in(0, 3)
            load_piece(1)
            load_piece(2)
            sp.dma_start(lora_a_raw, lora_a).then_inc(s_expand, 16)
            sp.dma_start(starts_i[:, :], starts.to_broadcast([P, 4])).then_inc(s_starts, 16)
            sp.dma_start(lora_b_stage, lora_b).then_inc(s_expand, 16)
            sp.dma_start(wr_raw, wr).then_inc(s_expand, 16)
            sp.dma_start(expand_stage, expand).then_inc(s_expand, 16)
            def group(g, first, last):
                for n in range(PIECES):
                    sp.wait_ge(s_piece_lo, g * PIECES + n + 1)
                    load_piece(n + SLOTS)
                    if n == 1 and first:
                        sp.wait_ge(s_const_hi, 5)
                        sp.wait_ge(s_const_lo, 3)
                        sp.wait_ge(s_p_ctx_bc, 1)
                        for t in range(NT):
                            load_x(0, t)
                    if n == 1 and not last:
                        sp.wait_ge(s_conv, g * GB + GB)
                        for t in range(NT):
                            load_conv_in(g + 1, t)
                    if n == 21:
                        store_half(g, 0)
                store_half(g, 1)
                if not last:
                    sp.wait_ge(s_stored, g * (16 * 2 * NT) + 16 * 2 * NT)
                    for t in range(NT):
                        load_x(g + 1, t)

            def store_half(g, h):
                for t in range(NT):
                    sp.wait_ge(s_out, g * 8 + 8 + h * NT + t + 1)
                    sp.dma_start(out[bass.ds(g, 1), t, :, h * HALF:(h + 1) * HALF].rearrange("a p n -> (a p) n"),
                                 x1[:, t, h * HALF:(h + 1) * HALF]).then_inc(s_stored, 16)

            group(0, True, False)
            with sp.Fori(1, GROUPS - 1) as g:
                group(g, False, False)
            group(GROUPS - 1, False, True)
            sp.wait_ge(s_stored, 16 * 2 * NT * GROUPS)
            for n in range(SLOTS):
                sp.wait_ge(s_raw[n], 16 * (GROUPS * PIECES // SLOTS + 1))

        @block.gpsimd
        def _(pool):
            pool.memset(ones[:, :], 1.0).then_inc(s_ones, 1)
            pool.memset(lora_a_r[:, :, :].bitcast(F32), 0.0).then_inc(s_ones, 1)
            pool.memset(lora_s2[:, :].bitcast(F32), 0.0).then_inc(s_ones, 1)
            pool.wait_ge(s_ones, 3)
            pool.memset(lora_s2[96:P, :].bitcast(F32), 1.0).then_inc(s_ones, 1)
            pool.wait_ge(s_ones, 4)
            pool.wait_ge(s_att, 4)
            pool.wait_ge(s_later, 16)
            for k in range(KC):
                weight = att_pair[:, :, k:k + 1].to_broadcast([P, NB // 2, C])
                matrix = mixw[:, k:k + 1, :].to_broadcast([P, NB // 2, C])
                if k == 0:
                    pool.tensor_tensor(agg[:, :, :], weight, matrix, ALU.mult).then_inc(s_agg, 1)
                else:
                    pool.tensor_tensor(agg_part, weight, matrix, ALU.mult).then_inc(s_agg, 1)
                    pool.wait_ge(s_agg, 2 * k)
                    pool.tensor_tensor(agg[:, :, :], agg[:, :, :], agg_part, ALU.add).then_inc(s_agg, 1)
                    pool.wait_ge(s_agg, 2 * k + 1)
            pool.wait_ge(s_const_lo, 3)
            pool.memset(blockdiag[:, :, :], 0.0).then_inc(s_ones, 1)
            pool.wait_ge(s_ones, 5)
            with pool.Fori(0, GROUPS) as g:
                pool.wait_ge(s_conv, g * GB + 1)
                for b in range(2):
                    rows = slice(b * C, (b + 1) * C)
                    pool.tensor_copy(blockdiag[rows, :, rows],
                                     agg[rows, bass.ds(g * NT, NT), :]).then_inc(s_bd, 1)

        @block.scalar
        def _(act):
            act.dma_start(consts1[:, :], first_consts).then_inc(s_first, 16)
            load_taps(act, 0)
            load_taps(act, 1)

            def hidden(n):
                act.wait_ge(s_p_hid, n + 1)
                if n == 0:
                    act.wait_ge(s_first, 32)
                act.activation(hid[:, n, :], banks[0][:, 0:NB], ACT.Gelu, bias=(b0s, b1s)[n]).then_inc(s_hid, 1)

            def spread_first():
                act.wait_ge(s_p_ctx_bc, 1)
                act.activation(cond_bc[:, 0:GB, :].rearrange("p b c -> p (b c)"), banks[1][:, :],
                               ACT.Copy).then_inc(s_ctx_bc, 1)

            def biases_out(n, ready, step, done):
                act.wait_ge(ready, step)
                act.dma_start(spread[n:n + 1, :].rearrange("a (b c) -> (a b) c", c=C), biases[:, n, :]).then_inc(done, 16)

            def biases_spread(n, to, b0, landed, done):
                act.wait_ge(landed, 16)
                act.dma_start(to[:, b0:, :].rearrange("p b c -> p (b c)"),
                              spread[n:n + 1, b0 * C:].to_broadcast([P, (NB - b0) * C])).then_inc(done, 16)

            def logits_exp():
                act.wait_ge(s_att, 1)
                act.activation(att[:, 0, :], banks[2][0:NB, 0:KC], ACT.Exp, bias=attstat[:, 0:1],
                               accum_out=attstat[:, 1:2]).then_inc(s_att_exp, 1)

            def const_hi(n):
                act.wait_ge(s_expand, 64)
                act.wait_ge(s_ones, 4)
                to, of = ((lora_a_r[:, :, 0:LORA], lora_a_raw), (lora_m1[:, :], lora_b_stage),
                          (lora_m2[0:LORA_LO, :], x1[0:LORA_LO, 1, :]), (wr_r[:, :, 0:KR_E], wr_raw),
                          (expand_r[:, :], expand_stage))[n]
                act.activation(to, of, ACT.Copy).then_inc(s_const_hi, 1)

            def first_after_conv(b):
                if b == 0:
                    hidden(1)
                if b == 2:
                    biases_out(0, s_ctx, 3, s_out_ctx)
                if b == 3:
                    logits_exp()
                if b in (3, 4, 5):
                    split_piece(0, b - 3)

            def split_piece(g, n):
                raw_landed(act, g, n)
                act.activation(piece_hi[:, n % SLOTS, :], raw[:, n % SLOTS, :], ACT.Copy).then_inc(s_piece_hi, 1)

            def next_piece(g, n):
                if 8 <= n < 16:
                    act.wait_ge(s_h, g * NCH + n - 7)
                elif n in (19, 23):
                    act.wait_ge(s_fin, g * 8 + n - 15)
                else:
                    act.wait_ge(s_piece_used, g * 14 + (n if n < 8 else n - 8 - (n > 19)) + 1)
                split_piece(g, n + SLOTS)

            def split_hi(g, item, to, of):
                act.wait_ge(s_ring, g * RING + item + 1)
                act.activation(to, of, ACT.Copy).then_inc(s_hi, 1)

            def group(g, first):
                if first:
                    hidden(0)
                    spread_first()
                for b in range(GB):
                    split_hi(g, CONV0 + b, u_conv(u_hi, b), ring_conv(CONV0 + b))
                    if first:
                        first_after_conv(b)
                if first:
                    for n in range(5):
                        const_hi(n)
                    biases_out(1, s_mixb, 3, s_out_mixb)
                next_piece(g, 0)
                if first:
                    biases_spread(1, mixb_bc, 0, s_out_mixb, s_mixb_bc)
                    biases_spread(0, cond_bc, GB, s_out_ctx, s_rest_bc)
                next_piece(g, 1)
                act.wait_ge(s_lora_masked, g + 1)
                act.activation(lora_s1[0:LORA_M, :], lora_h[0:LORA_M, :], ACT.Identity,
                               bias=ecol[0:LORA_M, 0:1]).then_inc(s_lora_s, 1)
                act.activation(lora_s2[LORA_LO:LORA_M, :], lora_h[0:LORA, :], ACT.Copy).then_inc(s_lora_s, 1)
                for n in range(2, 8):
                    next_piece(g, n)
                for c in range(NCH):
                    split_hi(g, MIX0 + c, v_hi[:, c, :], ring[:, (MIX0 + c) % SLOTS, :])
                act.wait_ge(s_score, g + 1)
                act.activation(score_t[:, :], banks[4][:, :], ACT.Copy).then_inc(s_score_t, 1)
                next_piece(g, 8)
                act.wait_ge(s_topk, 7 * g + 3)
                for t in range(NT):
                    act.activation(expd[:, t, :], left[:, 1, t, :], ACT.Exp,
                                   bias=stat[:, 0, t:t + 1]).then_inc(s_exp, 1)
                next_piece(g, 9)
                act.wait_ge(s_gate_t, g + 1)
                act.activation(gate_r[0:KR_E, :], banks[6][0:KR_E, :], ACT.Copy).then_inc(s_gate_hi, 1)
                next_piece(g, 10)

                def spread(c):
                    act.wait_ge(s_spread, g * NCH + c + 1)
                    if c >= 2:
                        act.wait_ge(s_ring, g * RING + H0 + c - 1)
                    act.activation(gate_x[:, c % 2, :], banks[(7, 5)[c % 2]][:, :], ACT.Copy).then_inc(s_gate_x, 1)

                for c in range(0, NCH, 2):
                    spread(c)
                    spread(c + 1)
                    for k in (c, c + 1):
                        split_hi(g, H0 + k, u_hi[:, k, :], ring[:, (H0 + k) % SLOTS, :])
                        if k != c or c == NCH - 2:
                            next_piece(g, 11 + c // 2 + (k == NCH - 1))
                for n in range(16, PIECES):
                    next_piece(g, n)

            group(0, True)
            with act.Fori(1, GROUPS) as g:
                group(g, False)

        @block.vector
        def _(dve):
            dve.wait_ge(s_ones, 4)
            dve.sem_inc(s_out, 8)


            def context():
                dve.wait_ge(s_first, 32)
                dve.wait_ge(s_p_ctx, 1)
                dve.tensor_scalar(ctx_t[0:C, :], banks[3][0:C, 0:GB], fs[0:C], None, ALU.add).then_inc(s_ctx, 1)
                dve.wait_ge(s_ctx, 1)
                dve.tensor_tensor(diag, ident[0:C, None, 0:C].to_broadcast([C, GB, C]),
                                  ctx_t[0:C, :, None].to_broadcast([C, GB, C]), ALU.mult).then_inc(s_ctx, 1)

            def rest_of_context():
                dve.wait_ge(s_p_ctx, 2)
                dve.tensor_copy(biases[:, 0, :], banks[2][0:NB, 0:C]).then_inc(s_ctx, 1)

            def softmax_max():
                dve.wait_ge(s_p_logit, 1)
                dve.tensor_reduce(attstat[:, 0:1], banks[2][0:NB, 0:KC], AX_X, ALU.max, negate=True).then_inc(s_att, 1)

            def softmax():
                dve.wait_ge(s_att_exp, 1)
                dve.reciprocal(attstat[:, 2:3], attstat[:, 1:2]).then_inc(s_att, 1)
                dve.wait_ge(s_att, 2)
                dve.tensor_scalar(att[:, 1, :], att[:, 0, :], attstat[:, 2:3], None, ALU.mult).then_inc(s_att, 1)
                dve.wait_ge(s_att, 3)
                dve.tensor_tensor(att_diag[0:NB], ident[0:NB, 0:NB, None].to_broadcast([NB, NB, KC]),
                                  att[:, 1, None, :].to_broadcast([NB, NB, KC]), ALU.mult).then_inc(s_mixb, 1)

            def mix_weights():
                dve.wait_ge(s_p_att, 1)
                dve.tensor_copy(att_t[0:KC, :], banks[0][0:KC, 0:NB]).then_inc(s_mixb, 1)
                dve.wait_ge(s_p_att, 2)
                both = banks[1][:, 0:NB * KC].rearrange("p (t b k) -> p t b k", b=2, k=KC)
                dve.tensor_copy(att_pair[0:C], both[0:C, :, 0, :])
                dve.tensor_copy(att_pair[C:P], both[C:P, :, 1, :]).then_inc(s_att, 1)

            def mix_bias():
                dve.wait_ge(s_p_att, 3)
                dve.tensor_copy(biases[:, 1, :], banks[4][0:NB, 0:C]).then_inc(s_mixb, 1)

            def adapters():
                step = 0

                def then(ins, wait=True):
                    nonlocal step
                    ins.then_inc(s_adapter, 1)
                    step += 1
                    if wait:
                        dve.wait_ge(s_adapter, step)

                dve.wait_ge(s_later, 16)
                dve.wait_ge(s_starts, 16)
                then(dve.tensor_copy(starts_f[:, :], starts_i[:, :]))
                for n in range(4):
                    then(dve.tensor_scalar(reached[:, n, :], brow, starts_f[:, n:n + 1], None, ALU.is_ge), n == 3)
                low, high = count[:, 0, :], count[:, 1, :]
                then(dve.tensor_scalar(low, reached[:, 0, :], -1.0, 2.0, ALU.mult, ALU.add))
                then(dve.tensor_tensor(low, low, reached[:, 1, :], ALU.mult))
                then(dve.tensor_tensor(low, low, reached[:, 0, :], ALU.add))
                then(dve.scalar_tensor_tensor(out=high, in0=reached[:, 3, :], scalar=3.0, in1=low,
                                              op0=ALU.add, op1=ALU.subtract))
                then(dve.tensor_tensor(high, high, reached[:, 2, :], ALU.mult))
                then(dve.tensor_tensor(high, high, low, ALU.add))
                then(dve.tensor_scalar(lora_mask[:, :], high, 2.0, acol, ALU.subtract, ALU.is_equal))

            def const_lo(n):
                dve.wait_ge(s_const_hi, (1, 2, 4)[n])
                to, of, hi = ((lora_a_r[:, :, LORA_LO:LORA_M], lora_a_raw, lora_a_r[:, :, 0:LORA]),
                              (lora_m2[LORA_LO:P, :], x1[LORA_LO:P, 1, :], lora_m1[LORA_LO:P, :]),
                              (wr_r[:, :, KR_E:P], wr_raw, wr_r[:, :, 0:KR_E]))[n]
                dve.tensor_tensor(to, of, hi.bitcast(F32), ALU.subtract).then_inc(s_const_lo, 1)

            def first_after_conv(b):
                if b == 0:
                    rest_of_context()
                if b == 3:
                    softmax_max()
                if b == 4:
                    softmax()
                if b == 6:
                    mix_weights()
                if b == 4:
                    split_piece(0, 0)

            def first_in_ffn0():
                split_piece(0, 1)
                for n in range(3):
                    const_lo(n)
                mix_bias()
                adapters()
                split_piece(0, 2)

            def split_piece(g, n):
                dve.wait_ge(s_piece_hi, g * PIECES + n + 1)
                dve.tensor_tensor(piece_lo[:, n % SLOTS, :], raw[:, n % SLOTS, :],
                                  piece_hi[:, n % SLOTS, :].bitcast(F32), ALU.subtract).then_inc(s_piece_lo, 1)

            def ring_free(g, item):
                dve.wait_ge(s_lo, g * RING + item + 1)

            def split_lo(g, item, to, of, hi):
                dve.wait_ge(s_hi, g * RING + item + 1)
                dve.tensor_tensor(to, of, hi, ALU.subtract).then_inc(s_lo, 1)

            dve.sem_inc(s_lo, SLOTS)

            def group(g, first):
                def conv_lo(b):
                    split_lo(g, CONV0 + b, u_conv(u_lo, b), ring_conv(CONV0 + b), u_conv(u_hi, b).bitcast(F32))

                for b in range(GB):
                    if first and b == 0:
                        context()
                    dve.wait_ge(s_conv, g * GB + b + 1)
                    if b == 0:
                        dve.wait_ge(s_ctx_bc, 1)
                    ring_free(g, CONV0 + b)
                    bias = cond_bc[:, bass.ds(g * GB + b, 1), :].rearrange("p a (g o) -> p (a g) o", g=CG)
                    dve.tensor_tensor(ring_conv(CONV0 + b),
                                      banks[4 + b % 4][:, :].rearrange("p (g j o) -> p g j o", g=CG, j=PH),
                                      bias[:, :, None, :].to_broadcast([P, CG, PH, CI]), ALU.add).then_inc(s_ring, 1)
                    if b:
                        conv_lo(b - 1)
                    if first:
                        first_after_conv(b)
                conv_lo(GB - 1)
                if first:
                    first_in_ffn0()
                split_piece(g, SLOTS)
                split_piece(g, SLOTS + 1)
                dve.wait_ge(s_lora_h, g + 1)
                mask = lora_mask[0:LORA_M, bass.ds(g * GB, GB)]
                dve.tensor_tensor(lora_h[0:LORA_M, :].rearrange("p (b c) -> p b c", b=GB),
                                  banks[4][0:LORA_M, :].rearrange("p (b c) -> p b c", b=GB),
                                  mask[:, :, None].to_broadcast([LORA_M, GB, C]), ALU.mult).then_inc(s_lora_masked, 1)
                dve.wait_ge(s_lora_s, 2 * g + 1)
                dve.wait_ge(s_lora_masked, g + 1)
                dve.tensor_tensor(lora_s2[0:LORA, :], lora_h[0:LORA, :], lora_s1[0:LORA, :].bitcast(F32),
                                  ALU.subtract).then_inc(s_lora_lo, 1)
                split_piece(g, 5)
                dve.wait_ge(s_x, g * (16 * NT) + 16 * NT)
                for h in range(2):
                    for t in range(NT):
                        dve.wait_ge(s_ffn, g * 8 + h * NT + t + 1)
                        half = x1[:, t, h * HALF:(h + 1) * HALF]
                        dve.tensor_tensor(half, half, banks[4 * h + t][:, :], ALU.add).then_inc(s_x1, 1)
                    for n in ((6, 7, 8, 9), ())[h]:
                        split_piece(g, n)

                if first:
                    dve.wait_ge(s_mixb_bc, 16)

                def mix_lo(c):
                    split_lo(g, MIX0 + c, v_lo[:, c, :], ring[:, (MIX0 + c) % SLOTS, :], v_hi[:, c, :].bitcast(F32))

                for c in range(NCH):
                    dve.wait_ge(s_mix, g * NCH + c + 1)
                    ring_free(g, MIX0 + c)
                    bias = mixb_bc[:, bass.ds(g * GB, GB), :].rearrange("p b c -> p (b c)")
                    dve.tensor_tensor(ring[:, (MIX0 + c) % SLOTS, :], banks[1 + c % 3][:, :], bias,
                                      ALU.add).then_inc(s_ring, 1)
                    if c >= 1:
                        mix_lo(c - 1)
                mix_lo(NCH - 1)
                split_piece(g, 10)
                dve.wait_ge(s_score_n, g + 1)
                scores = left[:, 1, :, :]
                dve.tensor_reduce(scores.rearrange("p t e -> p (t e)"),
                                  banks[5][:, :].rearrange("p (t a e) -> p t e a", t=NT, a=2), AX_X,
                                  ALU.add).then_inc(s_topk, 1)
                dve.wait_ge(s_topk, 7 * g + 1)
                settled(dve)
                for t in range(NT):
                    last = dve.max(top[:, t, 0:8], scores[:, t, :])
                last.then_inc(s_topk, 1)
                dve.wait_ge(s_topk, 7 * g + 2)
                dve.tensor_scalar(stat[:, 0, :], top[:, :, 0:1].rearrange("p t a -> p (t a)"), -1.0, None,
                                  ALU.mult).then_inc(s_topk, 1)
                settled(dve)
                for t in range(NT):
                    last = dve.match_replace(left[:, 0, t, :], top[:, t, 0:8], scores[:, t, :], NEG)
                last.then_inc(s_topk, 1)
                dve.wait_ge(s_topk, 7 * g + 4)
                settled(dve)
                for t in range(NT):
                    last = dve.max(top[:, t, 8:16], left[:, 0, t, :])
                last.then_inc(s_topk, 1)
                dve.wait_ge(s_exp, g * NT + NT)
                settled(dve)
                dve.wait_ge(s_topk, 7 * g + 5)
                settled(dve)
                for t in range(NT):
                    last = dve.match_replace(left[:, 1, t, :], top[:, t, 8:16], left[:, 0, t, :], NEG)
                last.then_inc(s_topk, 1)
                dve.wait_ge(s_topk, 7 * g + 6)
                for t in range(NT):
                    last = dve.scalar_tensor_tensor(out=expd[:, t, :], in0=left[:, 1, t, :], scalar=NEG,
                                                    in1=expd[:, t, :], op0=ALU.is_equal, op1=ALU.mult,
                                                    accum_out=stat[:, 1, t:t + 1])
                last.then_inc(s_topk, 1)
                dve.wait_ge(s_topk, 7 * g + 7)
                dve.reciprocal(stat[:, 2, :], stat[:, 1, :]).then_inc(s_recip, 1)
                dve.wait_ge(s_recip, g + 1)
                for t in range(NT):
                    dve.tensor_scalar(gate[:, t, :], expd[:, t, :], stat[:, 2, t:t + 1], 2.0, ALU.mult,
                                      ALU.mult).then_inc(s_gate, 1)
                split_piece(g, 11)
                split_piece(g, 12)
                dve.wait_ge(s_gate_t, g + 1)
                dve.wait_ge(s_gate_hi, g + 1)
                dve.tensor_tensor(gate_r[KR_E:P, :], banks[6][0:KR_E, :], gate_r[0:KR_E, :].bitcast(F32),
                                  ALU.subtract).then_inc(s_gate_lo, 1)
                split_piece(g, 13)

                def gated(c):
                    dve.wait_ge(s_h, g * NCH + c + 1)
                    dve.wait_ge(s_gate_x, g * NCH + c + 1)
                    ring_free(g, H0 + c)
                    dve.tensor_tensor(ring[:, (H0 + c) % SLOTS, :], banks[c % 4][:, :], gate_x[:, c % 2, :],
                                      ALU.mult).then_inc(s_ring, 1)

                for c in range(0, NCH, 2):
                    for k in (c, c + 1):
                        if c < NCH - 2:
                            gated(k)
                    for k in (c, c + 1):
                        if c == NCH - 2:
                            gated(k)
                        split_lo(g, H0 + k, u_lo[:, k, :], ring[:, (H0 + k) % SLOTS, :], u_hi[:, k, :].bitcast(F32))
                        if k != c or c == NCH - 2:
                            split_piece(g, 14 + c // 2 + (k == NCH - 1))
                for h in range(2):
                    for n in ((19, 20, 21), (22, 23, 24, 25))[h]:
                        split_piece(g, n)
                    for t in range(NT):
                        dve.wait_ge(s_fin, g * 8 + h * NT + t + 1)
                        half = x1[:, t, h * HALF:(h + 1) * HALF]
                        dve.tensor_tensor(half, half, banks[4 - 4 * h + t][:, :], ALU.add).then_inc(s_out, 1)
                split_piece(g, 26)

            group(0, True)
            dve.wait_ge(s_rest_bc, 16)
            with dve.Fori(1, GROUPS) as g:
                group(g, False)

        @block.tensor
        def _(pe):
            pe.wait_ge(s_ones, 1)
            for _ in range(WARM_UP):
                pe.matmul(banks[7][:, 0:P], ones[:, :], ones[:, :], start=True, stop=True)

            def context():
                pe.wait_ge(s_first, 16 * 2)
                pe.matmul(banks[3][0:C, 0:GB], cw_t, cond_t[:, 0:GB], start=True, stop=True).then_inc(s_p_ctx, 1)

            def hidden(n):
                if n:
                    pe.wait_ge(s_hid, 1)
                pe.matmul(banks[0][:, 0:NB], (w0s, w1s)[n], (cond_t, hid[:, 0, :])[n], start=True,
                          stop=True).then_inc(s_p_hid, 1)

            def rest_of_context():
                pe.matmul(banks[2][0:NB, 0:C], cond_t, cw_t, start=True, stop=False)
                pe.matmul(banks[2][0:NB, 0:C], ones[0:1, 0:NB], frow[0:1, :], start=False,
                          stop=True).then_inc(s_p_ctx, 1)

            def logits():
                pe.wait_ge(s_hid, 2)
                pe.wait_ge(s_ctx, 3)
                pe.matmul(banks[2][0:NB, 0:KC], hid[:, 1, :], w2s, start=True, stop=False)
                pe.matmul(banks[2][0:NB, 0:KC], ones[0:1, 0:NB], b2s[0:1, :], start=False,
                          stop=True).then_inc(s_p_logit, 1)

            def first_after_conv(b):
                if b == 0:
                    pe.wait_ge(s_ctx, 2)
                    pe.matmul(banks[1][:, :], ones[0:C, :], diag.rearrange("p b c -> p (b c)"), start=True,
                              stop=True).then_inc(s_p_ctx_bc, 1)
                if b == 1:
                    hidden(1)
                if b == 3:
                    logits()
                if b == 6:
                    pe.wait_ge(s_mixb, 1)
                    pe.transpose(banks[0][0:KC, 0:NB], att[:, 1, :], ident[0:NB, 0:NB]).then_inc(s_p_att, 1)
                    pe.wait_ge(s_ctx_bc, 1)
                    pe.matmul(banks[1][:, 0:NB * KC], ones[0:NB, :], att_diag[0:NB].rearrange("p b k -> p (b k)"),
                              start=True, stop=True).then_inc(s_p_att, 1)

            def mix_bias():
                pe.wait_ge(s_mixb, 2)
                pe.wait_ge(s_later, 16)
                pe.wait_ge(s_ring, CONV0 + 5)
                pe.matmul(banks[4][0:NB, 0:C], att_t[0:KC, :], mixb[0:KC, :], start=True, stop=True).then_inc(s_p_att, 1)

            def product(to, left_hi, left_lo, right_hi, right_lo, first, last):
                pe.matmul(to, left_hi, right_hi, start=first, stop=False)
                pe.matmul(to, left_hi, right_lo, start=False, stop=False)
                return pe.matmul(to, left_lo, right_hi, start=False, stop=last)

            def piece_ready(g, n):
                pe.wait_ge(s_piece_lo, g * PIECES + n + 1)

            def split_done(g, item):
                pe.wait_ge(s_lo, g * RING + item + 1 + SLOTS)

            def columns_piece(n, c):
                return (piece_hi[:, n % SLOTS, c * HALF:(c + 1) * HALF], piece_lo[:, n % SLOTS, c * HALF:(c + 1) * HALF])

            def group(g, first):
                if first:
                    context()
                    hidden(0)
                    rest_of_context()
                    pe.wait_ge(s_taps, 16 * CG)
                for b in range(GB):
                    if b % 2 == 0:
                        pe.wait_ge(s_convin[b // 2], g * 16 + 16)
                    if b < 4:
                        pe.wait_ge(s_out, g * 8 + b + 1)
                    else:
                        pe.wait_ge(s_ring, g * RING + CONV0 + b - 3)
                    for cg in range(CG):
                        for h in range(2):
                            mm = pe.matmul(banks[4 + b % 4][:, cg * P:(cg + 1) * P], conv_in[:, b, cg, h:h + Q],
                                           toep[:, cg, 1 - h, :], start=(h == 0), stop=(h == 1))
                    mm.then_inc(s_conv, 1)
                    if first:
                        first_after_conv(b)

                def ffn_piece(n):
                    h, j = n // 4, n % 4
                    piece_ready(g, n)
                    for t in range(NT):
                        if n == 0:
                            pe.wait_ge(s_out, g * 8 + 4 + t + 1)
                            split_done(g, CONV0 + 2 * t + 1)
                        for c in range(2):
                            k = 2 * j + c
                            mm = product(banks[4 * h + t][:, :], u_hi[:, k, t * P:(t + 1) * P],
                                         u_lo[:, k, t * P:(t + 1) * P], *columns_piece(n, c), k == 0, False)
                        if t == NT - 1:
                            mm.then_inc(s_piece_used, 1)
                        if j == 3:
                            lora_second(h, t)

                def lora_second(h, t):
                    if t == 0:
                        pe.wait_ge(s_lora_s, 2 * g + 2)
                        pe.wait_ge(s_lora_lo, g + 1)
                        if first and h == 0:
                            pe.wait_ge(s_const_hi, 3)
                            pe.wait_ge(s_const_lo, 2)
                    pe.matmul(banks[4 * h + t][:, :], lora_s1[0:LORA_M, t * P:(t + 1) * P],
                              lora_m1[0:LORA_M, h * HALF:(h + 1) * HALF], start=False, stop=False)
                    pe.matmul(banks[4 * h + t][:, :], lora_s2[0:LORA_M + 1, t * P:(t + 1) * P],
                              lora_m2[0:LORA_M + 1, h * HALF:(h + 1) * HALF], start=False,
                              stop=True).then_inc(s_ffn, 1)

                if first:
                    pe.wait_ge(s_att, 4)
                ffn_piece(0)
                if first:
                    mix_bias()
                ffn_piece(1)
                if first:
                    pe.wait_ge(s_mixb, 3)
                    pe.wait_ge(s_const_lo, 1)
                for k in range(NCH):
                    for part in (u_hi, u_lo):
                        mm = pe.matmul(banks[4][0:LORA_M, :], lora_a_r[:, k, :], part[:, k, :],
                                       start=(k == 0 and part is u_hi), stop=(k == NCH - 1 and part is u_lo))
                mm.then_inc(s_lora_h, 1)
                ffn_piece(2)
                ffn_piece(3)
                pe.wait_ge(s_lora_masked, g + 1)
                for n in (4, 5, 6, 7):
                    ffn_piece(n)

                def mix(c):
                    if c == 0:
                        pe.wait_ge(s_bd, 2 * g + 2)
                        pe.wait_ge(s_x1, g * 8 + 4)
                    if c == 4:
                        pe.wait_ge(s_x1, g * 8 + 8)
                    if c >= 3:
                        pe.wait_ge(s_ring, g * RING + MIX0 + c - 2)
                    for t in range(NT):
                        mm = pe.matmul(banks[1 + c % 3][:, t * P:(t + 1) * P], x1[:, t, c * P:(c + 1) * P],
                                       blockdiag[:, t, :], start=True, stop=True)
                    mm.then_inc(s_mix, 1)

                def score(c):
                    split_done(g, MIX0 + c)
                    if first and c == 0:
                        pe.wait_ge(s_const_lo, 3)
                    if c == 0:
                        pe.wait_ge(s_x1, g * 8 + 5)
                    pe.matmul(banks[4][:, :], wr_r[:, c, :], v_hi[:, c, :], start=(c == 0), stop=False)
                    mm = pe.matmul(banks[4][:, :], wr_r[:, c, :], v_lo[:, c, :], start=False, stop=(c == NCH - 1))
                    if c == NCH - 1:
                        mm.then_inc(s_score, 1)

                def h_part(c, ks):
                    n = 8 + c
                    if ks[0] == 0:
                        piece_ready(g, n)
                        if c >= 4:
                            pe.wait_ge(s_ring, g * RING + H0 + c - 3)
                    for k in ks:
                        if c == 0:
                            split_done(g, MIX0 + k)
                        cols = slice(k * P, (k + 1) * P)
                        mm = product(banks[c % 4][:, :], piece_hi[:, n % SLOTS, cols], piece_lo[:, n % SLOTS, cols],
                                     v_hi[:, k, :], v_lo[:, k, :], k == 0, k == NCH - 1)
                    if ks[-1] == NCH - 1:
                        mm.then_inc(s_h, 1)

                def spread(c):
                    if c == 0:
                        pe.wait_ge(s_gate_hi, g + 1)
                        pe.wait_ge(s_gate_lo, g + 1)
                    if c >= 2:
                        pe.wait_ge(s_gate_x, g * NCH + c - 1)
                    pe.matmul(banks[(7, 5)[c % 2]][:, :], expand_r[:, c * P:(c + 1) * P], gate_r[:, :],
                              start=True, stop=True).then_inc(s_spread, 1)

                for c in range(NCH + LAG):
                    if c < NCH:
                        mix(c)
                    if c >= LAG:
                        score(c - LAG)
                        h_part(0, (c - LAG,))
                h_part(1, (0,))
                pe.wait_ge(s_score_t, g + 1)
                for t in range(NT):
                    mm = pe.transpose(banks[5][:, t * P:(t + 1) * P], score_t[:, t * P:(t + 1) * P], ident)
                mm.then_inc(s_score_n, 1)
                front, back = (0, 1, 2, 3), (4, 5, 6, 7)
                h_part(1, (1, 2, 3) + back)
                h_part(2, front + back)
                for t in range(NT):
                    pe.wait_ge(s_gate, g * NT + t + 1)
                    settled(pe)
                    mm = pe.transpose(banks[6][0:KR_E, t * P:(t + 1) * P], gate[:, t, :], ident)
                mm.then_inc(s_gate_t, 1)
                for c in range(3, NCH):
                    h_part(c, front)
                    if c < 7:
                        spread(2 * (c - 3))
                        spread(2 * (c - 3) + 1)
                    h_part(c, back)

                for n in range(16, PIECES):
                    h, j = (n - 16) // 4, n % 4
                    piece_ready(g, n)
                    if n == 16:
                        pe.wait_ge(s_gate_x, g * NCH + NCH)
                    if h == 0:
                        split_done(g, H0 + 2 * j + 1)
                    for t in range(NT):
                        for c in range(2):
                            k = 2 * j + c
                            mm = product(banks[4 - 4 * h + t][:, :], u_hi[:, k, t * P:(t + 1) * P],
                                         u_lo[:, k, t * P:(t + 1) * P], *columns_piece(n, c), k == 0, k == NCH - 1)
                        if j < 3 and t == NT - 1:
                            mm.then_inc(s_piece_used, 1)
                        if j == 3:
                            mm.then_inc(s_fin, 1)

            group(0, True)
            with pe.Fori(1, GROUPS) as g:
                group(g, False)


def kernel(x, cond_128, fside_S_0, L0_cond_weight, L0_cond_c_weight, L0_ffn_weight, L0_ffn_bias,
           L0_ffn_lora_A, L0_ffn_lora_B, L0_ffn_lora_start_indices, L1_cond_W0, L1_cond_b0, L1_cond_W1,
           L1_cond_b1, L1_cond_W2, L1_cond_b2, L1_cond_weight, L1_cond_bias_k, L1_ffn_A, L1_ffn_B, L1_ffn_Wr):
    import numpy as np
    import concourse.bacc as bacc
    from concourse.bass_utils import run_bass_kernel_spmd

    x = np.asarray(x)
    padded = np.pad(x, ((0, 0), (0, 0), (TAPS // 2, TAPS // 2)))
    conv_x = padded.reshape(GROUPS, NT, 2, CG, CI, Q + 1, PH).transpose(0, 1, 6, 4, 2, 3, 5)[:, :, ::-1]
    taps = np.asarray(L0_cond_weight).reshape(CG, CI, CI, TAPS).transpose(0, 2, 3, 1)[:, :, ::-1, :]
    taps = np.pad(taps, ((0, 0), (0, 0), (PH - 1, PH - 1), (0, 0)))
    w = np.asarray(L0_ffn_weight).reshape(2, HALF, Q, 4, 2).transpose(0, 3, 2, 4, 1).reshape(8, P, L)
    a = np.asarray(L1_ffn_A).reshape(NCH, P, NCH, P).transpose(0, 3, 2, 1).reshape(8, P, L)
    b = (np.asarray(L1_ffn_B).transpose(0, 2, 1).reshape(4, 2, P, 2, HALF)
         .transpose(3, 0, 2, 1, 4).reshape(8, P, L))
    eye = np.eye(P, dtype=np.float32)
    rows = np.arange(P)
    adapter = (rows % LORA_LO) // RANK

    def side_by_side(names, parts):
        for (name, width), part in zip(names, parts, strict=True):
            assert part.shape[1] == width, name
        return np.concatenate([np.pad(v, ((0, P - v.shape[0]), (0, 0))) for v in parts], axis=1)

    mix_w = np.asarray(L1_cond_weight).reshape(KC, C, C).transpose(2, 0, 1).reshape(C, KC * C)
    adapters = np.asarray(L0_ffn_lora_B).transpose(0, 2, 1).reshape(LORA, L)
    adapters = np.pad(np.concatenate([adapters, np.asarray(L0_ffn_bias).reshape(1, L)]),
                      ((0, LORA_LO - LORA - 1), (0, 0)))
    arrays = {
        "conv_x": conv_x.reshape(GROUPS, NT, P, 2 * CG * (Q + 1)),
        "x": x.reshape(GROUPS, NT, P, L),
        "taps": taps,
        "pieces": np.concatenate([w, a, b]),
        "first_consts": side_by_side(FIRST, [
            eye, np.asarray(cond_128).T, np.asarray(L0_cond_c_weight).T, np.asarray(fside_S_0).reshape(C, 1),
            np.asarray(fside_S_0).reshape(1, C),
            np.asarray(L1_cond_b0).reshape(P, 1), np.asarray(L1_cond_b1).reshape(P, 1),
            np.asarray(L1_cond_W2), np.asarray(L1_cond_b2).reshape(1, KC)]),
        "hidden_w": np.concatenate([np.asarray(L1_cond_W0), np.asarray(L1_cond_W1)], axis=1),
        "later_consts": side_by_side(LATER, [
            np.asarray(L1_cond_bias_k), np.tile(np.arange(NB, dtype=np.float32), (P, 1)),
            adapter.astype(np.float32).reshape(P, 1), (rows == LORA).astype(np.float32).reshape(P, 1),
            np.concatenate([mix_w, mix_w])]),
        "lora_a": np.asarray(L0_ffn_lora_A).reshape(LORA, Q, PH).transpose(1, 2, 0),
        "lora_b": np.concatenate([adapters, adapters]),
        "starts": np.asarray(L0_ffn_lora_start_indices).reshape(1, 4),
        "wr": np.asarray(L1_ffn_Wr).reshape(KR_E, NCH, P).transpose(2, 1, 0),
        "expand": np.tile(np.repeat(np.eye(KR_E, dtype=np.float32), RANK, axis=1), (2, 1)),
    }
    nc = bacc.Bacc("TRN2", target_bir_lowering=False, num_devices=1)
    aps = {}
    for name, v in arrays.items():
        arrays[name] = v = np.ascontiguousarray(v)
        aps[name] = nc.dram_tensor(name, v.shape, mybir.dt.from_np(v.dtype), kind="ExternalInput").ap()
    out = nc.dram_tensor("out", (GROUPS, NT, P, L), F32, kind="ExternalOutput").ap()
    spread = nc.dram_tensor("spread", (2, NB * C), F32, kind="Internal").ap()
    adaln_ffn_kernel(nc, **aps, spread=spread, out=out)
    result = run_bass_kernel_spmd(nc, [arrays], core_ids=[0]).results[0]["out"]
    return result.reshape(NB, C, L)
```
